# Optimizing a Trainium2 kernel written in Bass

```python
import numpy as np
import jax
import jax.numpy as jnp

def _softmax(x, axis=-1):
    return jax.nn.softmax(x, axis=axis)

def _gelu(x):
    return jax.nn.gelu(x, approximate=True)

def _silu(x):
    return jax.nn.silu(x)

def _sigmoid(x):
    return jax.nn.sigmoid(x)

def _layernorm(x, axis=-1, eps=1e-05):
    m = jnp.mean(x, axis=axis, keepdims=True)
    v = jnp.var(x, axis=axis, keepdims=True)
    return (x - m) / jnp.sqrt(v + eps)

def _scatter_add(tgt, idx, src, axis=0):
    return tgt.at[idx].add(src)

def _segment_sum(src, seg, n):
    return jax.ops.segment_sum(src, seg, n)
kernel_name = 'mk_conv_preact_d2_conv_nchw256_r2_78ec61'

def setup_inputs(seed: int=0):
    np.random.seed(seed)
    _w = jnp.asarray

    def _rec_inputs():
        import jax
        import jax.numpy as jnp
        _gk = jax.random.key(seed)
        x = -0.0003929 + 0.9999 * jax.random.normal(jax.random.fold_in(_gk, 1), (16, 128, 32, 32), jnp.float32)
        return x
    x = _rec_inputs()

    def _L0_conv_setup():
        import math
        import jax, jax.numpy as jnp
        from jax import lax
        import numpy as np
        DN = ('NCHW', 'OIHW', 'NCHW')
        key = jax.random.key(seed)
        k0, k1, k2, k3, k4, k5 = jax.random.split(key, 6)
        n, c, h, w = (16, 128, 32, 32)
        x = jax.random.normal(k0, (n, c, h, w), jnp.float32)
        b1 = math.sqrt(3.0 / h)
        p1 = jax.random.uniform(k1, (h, c // 8), jnp.float32, -b1, b1)
        p3 = jax.random.normal(k2, (c, 1, 9, 9), jnp.float32) * 0.05
        p4 = jax.random.normal(k3, (c, 4, 5, 1), jnp.float32) * 0.05
        b5 = math.sqrt(3.0 / (c * w // 8))
        p5 = jax.random.uniform(k4, (c // 8, w, 1, 3 * c), jnp.float32, -b5, b5)
        p6 = jax.random.normal(k5, (c, 1, 1, 3), jnp.float32) * 0.3
        return {'x': x, 'p1': p1, 'p3': p3, 'p4': p4, 'p5': p5, 'p6': p6}
    _L0_conv_all = _L0_conv_setup()
    _L0_conv_in = {k: v for k, v in _L0_conv_all.items() if k in ('p1', 'p3', 'p4', 'p5', 'p6')}
    del _L0_conv_all

    def _L1_conv_setup():
        import jax, jax.numpy as jnp
        import numpy as np
        BN_EPS = 1e-05

        def _haar_details(x):
            B, C, H, W = x.shape
            xb = x.reshape(B, C, H // 2, 2, W // 2, 2)
            p = xb[:, :, :, 0, :, 0]
            q = xb[:, :, :, 0, :, 1]
            r = xb[:, :, :, 1, :, 0]
            s = xb[:, :, :, 1, :, 1]
            cH = (p + q - r - s) * 0.5
            cV = (p - q + r - s) * 0.5
            cD = (p - q - r + s) * 0.5
            return (cH, cV, cD)
        key = jax.random.key(seed)
        k1, k2 = jax.random.split(key)
        B, C, H, W = (8, 128, 64, 64)
        x = jax.random.normal(k1, (B, C, H, W), dtype=jnp.float32)
        conv_w = jax.random.normal(k2, (C, 4 * C), dtype=jnp.float32) * (1.0 / np.sqrt(4 * C))
        gamma = jnp.ones((C,), dtype=jnp.float32)
        beta = jnp.zeros((C,), dtype=jnp.float32)
        return {'x': x, 'conv_w': conv_w, 'gamma': gamma, 'beta': beta}
    _L1_conv_all = _L1_conv_setup()
    _L1_conv_in = {k: v for k, v in _L1_conv_all.items() if k in ('conv_w', 'gamma', 'beta')}
    del _L1_conv_all
    return {'x': x, 'L0_conv_p1': _L0_conv_in['p1'], 'L0_conv_p3': _L0_conv_in['p3'], 'L0_conv_p4': _L0_conv_in['p4'], 'L0_conv_p5': _L0_conv_in['p5'], 'L0_conv_p6': _L0_conv_in['p6'], 'L1_conv_conv_w': _L1_conv_in['conv_w'], 'L1_conv_gamma': _L1_conv_in['gamma'], 'L1_conv_beta': _L1_conv_in['beta']}

def reference(x, L0_conv_p1, L0_conv_p3, L0_conv_p4, L0_conv_p5, L0_conv_p6, L1_conv_conv_w, L1_conv_gamma, L1_conv_beta):
    import jax
    import jax.numpy as jnp

    def _L0_conv_ref(x, p1, p3, p4, p5, p6):
        import math
        import jax, jax.numpy as jnp
        from jax import lax
        import numpy as np
        DN = ('NCHW', 'OIHW', 'NCHW')
        n, c, h, w = x.shape
        t1 = jnp.einsum('nchw,he->ncew', x, p1)
        xp = jnp.pad(x, ((0, 0), (0, 0), (1, 1), (0, 0)))
        t2 = jnp.stack([xp[:, :, k:k + h, :] for k in range(3)], axis=2)
        t3 = lax.conv_general_dilated(t1, p3, (1, 1), ((4, 4), (4, 4)), dimension_numbers=DN, feature_group_count=c)
        t4 = lax.conv_general_dilated(t3, p4, (1, 1), ((2, 2), (0, 0)), dimension_numbers=DN, feature_group_count=c // 4)
        t5 = jnp.einsum('ncew,ewf->ncf', t4, p5[:, :, 0, :])
        t6 = lax.conv_general_dilated(t5[:, :, None, :], p6, (1, 1), ((0, 0), (1, 1)), dimension_numbers=DN, feature_group_count=c)[:, :, 0, :]
        out = jnp.einsum('ncf,nfp->ncp', t6, t2.reshape(n, 3 * c, h * w))
        return (out / math.sqrt(3 * c)).reshape(n, c, h, w)

    def _L1_conv_ref(x, conv_w, gamma, beta):
        import jax, jax.numpy as jnp
        import numpy as np
        BN_EPS = 1e-05

        def _haar_details(x):
            B, C, H, W = x.shape
            xb = x.reshape(B, C, H // 2, 2, W // 2, 2)
            p = xb[:, :, :, 0, :, 0]
            q = xb[:, :, :, 0, :, 1]
            r = xb[:, :, :, 1, :, 0]
            s = xb[:, :, :, 1, :, 1]
            cH = (p + q - r - s) * 0.5
            cV = (p - q + r - s) * 0.5
            cD = (p - q - r + s) * 0.5
            return (cH, cV, cD)
        B, C, H, W = x.shape
        xs = jax.lax.stop_gradient(x)
        cH, cV, cD = _haar_details(xs)
        up = lambda t: jax.image.resize(t, (B, C, H, W), method='bilinear')
        enhanced = jnp.concatenate([x, up(cH), up(cV), up(cD)], axis=1)
        y = jnp.einsum('bchw,oc->bohw', enhanced, conv_w)
        mean = jnp.mean(y, axis=(0, 2, 3), keepdims=True)
        var = jnp.mean((y - mean) ** 2, axis=(0, 2, 3), keepdims=True)
        y_hat = (y - mean) * jax.lax.rsqrt(var + BN_EPS)
        out = jax.nn.relu(y_hat * gamma[None, :, None, None] + beta[None, :, None, None])
        return out

    def _gn(v, G=32, eps=1e-05):
        B_, C_, H_, W_ = v.shape
        g = v.reshape(B_, G, C_ // G, H_, W_)
        m = jnp.mean(g, axis=(2, 3, 4), keepdims=True)
        s = jnp.var(g, axis=(2, 3, 4), keepdims=True)
        return ((g - m) / jnp.sqrt(s + eps)).reshape(v.shape)

    def _ln_c(v, eps=1e-06):
        m = jnp.mean(v, axis=1, keepdims=True)
        s = jnp.var(v, axis=1, keepdims=True)
        return (v - m) / jnp.sqrt(s + eps)

    def _ln_t(v, eps=1e-05):
        m = jnp.mean(v, axis=-1, keepdims=True)
        s = jnp.var(v, axis=-1, keepdims=True)
        return (v - m) / jnp.sqrt(s + eps)

    def _to_tokens(v):
        B_, C_, H_, W_ = v.shape
        return v.reshape(B_, C_, H_ * W_).transpose(0, 2, 1)

    def _from_tokens(t, like):
        B_, C_, H_, W_ = like.shape
        return t.transpose(0, 2, 1).reshape(B_, C_, H_, W_)
    x = x + _L0_conv_ref(_gn(x), L0_conv_p1, L0_conv_p3, L0_conv_p4, L0_conv_p5, L0_conv_p6)
    x = x + _L1_conv_ref(_gn(x), L1_conv_conv_w, L1_conv_gamma, L1_conv_beta)
    return x

_drawn_inputs = setup_inputs


def setup_inputs(seed=0):
    import zlib

    import numpy as np

    out = dict(_drawn_inputs(seed))
    spreads = {'L1_conv_gamma': (1.0, 0.2), 'L1_conv_beta': (0.0, 0.1)}
    factors = {}
    for name, (base, spread) in spreads.items():
        noise = np.random.default_rng([zlib.crc32(name.encode()), seed]).standard_normal(out[name].shape)
        drawn = base * np.exp(spread * noise) if base else spread * noise
        out[name] = jnp.asarray(drawn.astype(out[name].dtype))
    for name, factor in factors.items():
        out[name] = (out[name] * factor).astype(out[name].dtype)
    return out
```

```python
import concourse.bass as bass
from concourse import mybir
from contextlib import ExitStack

F32 = mybir.dt.float32
ALU = mybir.AluOpType
ACT = mybir.ActivationFunctionType

N, C, H, W = 16, 128, 32, 32
HW = H * W
CI = 4
G = C // CI
E = 16
KD, KX = 9, 9
K4 = 5
NF = 3 * C
J = W // 2
JP = J + 4
NO = N + 1
TAPS = 5
SHIFTS = 2 * TAPS
NB, GB = 4, 8
JC, JL = 4, 4
GN_EPS = 1e-5
BN_EPS = 1e-5
HALF = HW // 2
ZP = J + 2


def build(nc, x, p1, p3, p4, p5, p6, conv_w, gamma, beta, out):
    ctx = ExitStack()
    with ctx:
        def sb(name, shape):
            return ctx.enter_context(nc.sbuf_tensor(name, shape, F32))

        def sem(name):
            return ctx.enter_context(nc.semaphore(name))

        x_sb = sb("x_sb", [128, N, HW])
        y_sb = sb("y_sb", [128, N, HW])
        y_flat = y_sb[:, :, :].rearrange("p n f -> p (n f)")
        n_t1 = G * JP * NO
        t1 = y_flat[:, 0:n_t1].rearrange("p (g j n) -> p g j n", g=G, j=JP)
        toe3 = y_flat[:, n_t1:n_t1 + G * SHIFTS * E].rearrange("p (g s m) -> p g s m", g=G, s=SHIFTS)

        DB = CI * JC * GB * NO
        d_sb = sb("d_sb", [128, NB, CI, JC * GB * NO])
        d_flat = d_sb[:, :, :, :].rearrange("p b c r -> p (b c r)")
        at = [0]

        def setup(n):
            at[0] += n
            return d_flat[:, at[0] - n:at[0]]

        xa = setup(2 * HW).rearrange("p (b w g) -> p b w g", b=2, g=G)
        ones_row = setup(HALF)
        p3_rows = setup(G * 11).rearrange("p (g s) -> p g s", g=G)
        p4_rows = setup(C).rearrange("p (g c) -> p g c", g=G)
        p4_raw = setup(CI * K4)
        sel_half = setup(2 * E * CI * E).rearrange("p (s m c e) -> p s m c e", s=2, m=E, c=CI)
        p5_raw = setup(JC * NF).rearrange("p (j f) -> p j f", j=JC)
        w_perm = setup(4 * C).rearrange("p (k c) -> p k c", k=4)
        p1_blk = setup(CI * E)
        w_raw = setup(4 * C)
        mask8 = setup(8)
        w_det = setup(3 * C).rearrange("p (k c) -> p k c", k=3)

        arena = sb("arena", [128, 8480])
        at2 = [0]

        def stage2(n):
            at2[0] += n
            return arena[:, at2[0] - n:at2[0]]

        sel = arena[:, 0:2 * E * 128].rearrange("p (s m v q) -> p s m v q", s=2, m=E, v=2)
        t4_out = stage2(2 * J * GB * NO).rearrange("p (b jl jc g n) -> p b jl jc g n", b=2, jl=JL, jc=JC, g=GB)
        t4_send = t4_out.rearrange("p b jl jc g n -> p b jl (jc g n)")
        s3 = stage2(2 * SHIFTS * CI * E).rearrange("p (b s c m) -> p b s c m", b=2, s=SHIFTS, c=CI)
        toe4 = stage2(G * CI * E).rearrange("p (g c m) -> p g c m", g=G, c=CI)
        s4 = stage2(2 * 128).rearrange("p (b v m) -> p b v m", b=2, v=2)
        t3_sb = stage2(2 * J * NO).rearrange("p (b f) -> p b f", b=2)
        at3 = [0]

        def stage3(n):
            at3[0] += n
            return arena[:, at3[0] - n:at3[0]]

        g1 = stage3(2 * (H + 2) * W).rearrange("p (b f) -> p b f", b=2)
        u_sb = stage3(2 * NF).rearrange("p (b f) -> p b f", b=2)
        t6t = stage3(2 * NF).rearrange("p (b k c) -> p b k c", b=2, k=3)
        dn = stage3(2 * JC * C).rearrange("p (b j c) -> p b j c", b=2, j=JC)
        zp = stage3(2 * J * ZP).rearrange("p (b i j) -> p b i j", b=2, i=J)
        z3 = stage3(2 * J * J).rearrange("p (b i j) -> p b i j", b=2, i=J)
        zh = stage3(2 * ZP * W).rearrange("p (b i w) -> p b i w", b=2, i=ZP)

        q6 = stage3(NF)
        p5_sb = sb("p5_sb", [128, JC, NF])
        ident = sb("ident", [128, 128])
        g_mean = sb("g_mean", [128, 4, G])
        ci_mask = sb("ci_mask", [128, CI])
        v_mask = sb("v_mask", [128, 2])
        w_t = sb("w_t", [128, 5, C])
        p6_sb = sb("p6_sb", [128, 3])
        a6 = sb("a6", [128, 3, N])
        gb = sb("gb", [128, 2])
        mv1 = sb("mv1", [128, N, 2])
        gs1 = sb("gs1", [128, N, 2])
        rs1 = sb("rs1", [128, 3, N])
        st2 = sb("st2", [128, 2, 12])
        mv2 = sb("mv2", [128, 2, 2])
        gs2 = sb("gs2", [128, 2, 2])
        rs2 = sb("rs2", [128, 2, 5])
        sty = sb("sty", [128, N, 12])
        st1 = sty
        fin = sb("fin", [128, 8])
        eps = sb("eps", [128, 1])

        bank = [ctx.enter_context(nc.psum_tensor(f"bank{i}", [128, 512], F32)) for i in range(4)]
        wide = [ctx.enter_context(nc.psum_tensor(f"wide{i}", [128, 1024], F32)) for i in range(2)]
        ps_t1 = [bank[0], bank[1]]
        ps_sel = [bank[2], bank[3]]
        ps_t3 = [wide[0][:, 0:J * NO], wide[0][:, 512:512 + J * NO]]
        ps_t4 = [wide[1][:, 0:J * NO], wide[1][:, 512:512 + J * NO]]
        ps_t5, ps_t6, ps_z, ps_st = bank
        ps_o, ps_y = wide

        names = ("p1_in w_det sel p5_pm w_pm x_in w_in const zeros sel_rows xa t1_mm t1_ev sel_mm sel_ev tr_w p4_tr p4_ev "
                 "s3 conv t3_ev t4_mm t4_ev d_in st1 gst_mm gst gst_q rs1 "
                 "dn t5 u_act u t6_mm t6_ev g1 o_mm x1 st2 st2_mm st2_v st2_q st2_r g2 y_mm z_mm z_ev zh y "
                 "fin_s fin_q fin relu res dve pool stored dve_o0 y_rd sty").split()
        s = {n: sem("s_" + n) for n in names}
        x_in = [sem(f"s_x_in{k}") for k in range(N // 2)]
        d_in = [sem(f"s_d_in{b}") for b in range(NB)]

        def chained(eng, name):
            count = [0]

            def link(ins):
                count[0] += 1
                ins.then_inc(s[name], 1)
                eng.wait_ge(s[name], count[0])
            return link

        block = ctx.enter_context(nc.Block())

        @block.sync
        def _(sp):
            for n in range(0, N, 2):
                for ci in range(CI):
                    sp.dma_start(x_sb[G * ci:G * ci + G, n:n + 2, :],
                                 x[n:n + 2].rearrange("n (g c) h w -> c g n (h w)", c=CI)[ci]
                                 ).then_inc(x_in[n // 2], 16)
            for b in range(NB):
                sp.wait_ge(s["t4_ev"], GB * (b + 1))
                if b == 0:
                    sp.wait_ge(s["t1_ev"], NO)
                    sp.wait_ge(s["sel_ev"], 36)
                    sp.wait_ge(s["tr_w"], 1)
                    sp.wait_ge(s["p5_pm"], 1)
                    sp.wait_ge(s["w_det"], 1)
                for jl in range(JL):
                    for v in range(2):
                        for co in range(CI):
                            src, dst = 64 * v + E * co, 32 * jl + E * v
                            sp.dma_start(d_sb[dst:dst + E, b, co, :],
                                         t4_send[src:src + E, b % 2, jl, :]).then_inc(d_in[b], 16)
            for n in range(N):
                sp.wait_ge(s["res"], n + 1)
                for ci in range(CI):
                    sp.dma_start(out[n].rearrange("(g c) h w -> c g (h w)", c=CI)[ci],
                                 x_sb[G * ci:G * ci + G, n, :]).then_inc(s["stored"], 16)
            sp.wait_ge(s["stored"], 16 * CI * N)

        @block.gpsimd
        def _(pool):
            link = chained(pool, "pool")
            link(pool.memset(p1_blk, 0.0))
            pool.memset(ones_row, 1.0)
            pool.memset(p3_rows[0:CI * KD], 0.0)
            pool.memset(eps[:, :], GN_EPS)
            pool.memset(t1[:, :, 0:2, :], 0.0)
            pool.memset(t1[:, :, JP - 2:JP, :], 0.0).then_inc(s["zeros"], 1)
            pool.memset(sel_half[0:CI * KD], 0.0)
            pool.memset(ident[:, :], 0.0)
            pool.memset(mask8, 1.0)
            pool.memset(v_mask[:, :], 1.0)
            link(pool.memset(g_mean[:, :, :], 0.0))
            for i, (k, half) in enumerate(((KD, KD // 2), (K4, K4 // 2))):
                v = sel_half[0:CI * k, i]
                link(pool.affine_select(out=v, in_=v, compare_op=ALU.not_equal, fill=1.0, base=-half,
                                        pattern=[[1, E], [-k, CI], [-1, E]], channel_multiplier=1))
                link(pool.affine_select(out=v, in_=v, compare_op=ALU.is_ge, fill=0.0, base=half,
                                        pattern=[[-1, E], [0, CI], [1, E]], channel_multiplier=0))
                link(pool.affine_select(out=v, in_=v, compare_op=ALU.is_ge, fill=0.0, base=k - 1 - half,
                                        pattern=[[1, E], [0, CI], [-1, E]], channel_multiplier=0))
                src = v.rearrange("p m c e -> p m (c e)").unsqueeze(2).broadcast_to([CI * k, E, 2, CI * E])
                pool.tensor_copy(sel[0:CI * k, i], src).then_inc(s["sel"], 1)
            pool.affine_select(out=ident[:, :], in_=ident[:, :], compare_op=ALU.not_equal, fill=1.0,
                               base=0, pattern=[[-1, 128]], channel_multiplier=1)
            for m in range(CI):
                link(pool.affine_select(out=g_mean[:, :, :], in_=g_mean[:, :, :], compare_op=ALU.not_equal,
                                        fill=1.0 / CI, base=-G * m, pattern=[[0, CI], [-1, G]],
                                        channel_multiplier=1))
            link(pool.affine_select(out=mask8, in_=mask8, compare_op=ALU.is_ge, fill=0.0, base=0,
                                    pattern=[[-16, 8]], channel_multiplier=1))
            link(pool.affine_select(out=mask8, in_=mask8, compare_op=ALU.is_ge, fill=0.0, base=15,
                                    pattern=[[16, 8]], channel_multiplier=-1))
            link(pool.tensor_tensor(ci_mask[:, :], mask8[:, 0:4], mask8[:, 4:8], ALU.add))
            link(pool.affine_select(out=v_mask[:, :], in_=v_mask[:, :], compare_op=ALU.is_ge, fill=0.0, base=63,
                                    pattern=[[128, 2]], channel_multiplier=-1))
            link(pool.affine_select(out=v_mask[:, :], in_=v_mask[:, :], compare_op=ALU.is_ge, fill=0.0, base=64,
                                    pattern=[[-128, 2]], channel_multiplier=1))
            pool.memset(fin[:, 0:1], 0.0).then_inc(s["const"], 1)
            pool.wait_ge(s["w_in"], 16 * 24)
            pool.tensor_copy(w_perm.rearrange("p k (c g) -> p k c g", c=CI),
                             w_raw.rearrange("p (k g c) -> p k c g", k=4, c=CI)).then_inc(s["w_pm"], 1)
            for jc in range(JC):
                last = pool.tensor_copy(p5_sb[:, jc, :].rearrange("p (k c g) -> p k c g", k=3, c=CI),
                                        p5_raw[:, jc, :].rearrange("p (g c k) -> p k c g", c=CI, k=3))
            last.then_inc(s["p5_pm"], 1)
            pool.wait_ge(s["sel_ev"], 36)
            for g in range(G):
                if g >= 2:
                    pool.wait_ge(s["conv"], g - 1)
                    pool.wait_ge(s["t4_mm"], g - 1)
                pool.tensor_tensor(
                    s3[:, g % 2], toe3[:, g].unsqueeze(2).broadcast_to([128, SHIFTS, CI, E]),
                    ci_mask[:, :].unsqueeze(1).unsqueeze(3).broadcast_to([128, SHIFTS, CI, E]), ALU.mult)
                pool.tensor_tensor(
                    s4[:, g % 2], toe4[:, g].rearrange("p c m -> p (c m)").unsqueeze(1).broadcast_to([128, 2, CI * E]),
                    v_mask[:, :].unsqueeze(2).broadcast_to([128, 2, CI * E]), ALU.mult).then_inc(s["s3"], 1)
            pool.wait_ge(s["conv"], G)
            pool.wait_ge(s["t4_mm"], G)
            for b in range(NB):
                pool.wait_ge(d_in[b], 16 * 2 * JL * CI)

            def take_sample(n, k):
                if k >= 2:
                    pool.wait_ge(s["t5"], k - 1)
                src = d_sb[:, :, :, :].rearrange("p b c (j g n) -> p j c b g n", j=JC, n=NO)
                for jc in range(JC):
                    last = pool.tensor_copy(dn[:, k % 2, jc, :].rearrange("p (c b g) -> p c b g", c=CI, b=NB),
                                            src[:, jc, :, :, :, n])
                last.then_inc(s["dn"], 1)

            v = g1.rearrange("p b (i w) -> p b i w", w=W)
            pool.memset(v[:, :, 0:H + 2:H + 1, :], 0.0).then_inc(s["zeros"], 1)
            take_sample(N, 0)
            take_sample(0, 1)
            for t in range(N + 2):
                if t + 1 < N:
                    take_sample(t + 1, t + 2)
                n = t - 2
                if n >= 0:
                    pool.wait_ge(s["z_ev"], n + 1)
                    if n >= 2:
                        pool.wait_ge(s["y"], n - 1)
                    rows = zh[:, n % 2, 1:J + 1, :].rearrange("p i (j a) -> p i j a", a=2)
                    pool.tensor_tensor(rows[:, :, :, 0], z3[:, n % 2], zp[:, n % 2, :, 0:J], ALU.add)
                    link(pool.tensor_tensor(rows[:, :, :, 1], z3[:, n % 2], zp[:, n % 2, :, 2:ZP], ALU.add))
                    pool.tensor_copy(zh[:, n % 2, 0:ZP:ZP - 1, :],
                                     zh[:, n % 2, 1:J + 1:J - 1, :]).then_inc(s["zh"], 1)

        @block.scalar
        def _(act):
            act.wait_ge(s["pool"], 1)
            for ci in range(CI):
                act.dma_start(p1_blk[32 * ci:32 * ci + 32, E * ci:E * ci + E], p1).then_inc(s["p1_in"], 16)
            act.wait_ge(s["zeros"], 1)
            for ci in range(CI):
                act.dma_start(p3_rows[KD * ci:KD * ci + KD, :, 1:1 + KX],
                              p3.rearrange("(g c) o y x -> c y g (o x)", c=CI)[ci]).then_inc(s["sel_rows"], 16)
            act.dma_start(p4_raw, p4.rearrange("c i y x -> c (i y x)")).then_inc(s["sel_rows"], 16)
            for ci in range(CI):
                q = slice(G * ci, G * ci + G)
                act.dma_start(w_raw[q], conv_w.rearrange("(g c) f -> c g f", c=CI)[ci]).then_inc(s["w_in"], 16)
                act.dma_start(p6_sb[q, :], p6.rearrange("(g c) a b d -> c g (a b d)", c=CI)[ci]).then_inc(s["w_in"], 16)
                act.dma_start(gb[q, 0:1], gamma.rearrange("(g c a) -> c g a", c=CI, a=1)[ci],
                              allow_slow_non_contiguous=True).then_inc(s["w_in"], 16)
                act.dma_start(gb[q, 1:2], beta.rearrange("(g c a) -> c g a", c=CI, a=1)[ci],
                              allow_slow_non_contiguous=True).then_inc(s["w_in"], 16)
            for jl in range(JL):
                for v in range(2):
                    act.dma_start(p5_raw[32 * jl + 16 * v:32 * jl + 16 * v + 16, :, :],
                                  p5.rearrange("e (j r) o f -> r e j (o f)", r=2 * JL)[2 * jl + 1 - v]
                                  ).then_inc(s["w_in"], 16)

            def t1_evacuate(n):
                act.wait_ge(s["t1_mm"], n + 1)
                act.copy(t1[:, :, 2:2 + J, n].rearrange("p g j -> p j g"),
                         ps_t1[n % 2][:, :].rearrange("p (j g) -> p j g", g=G)).then_inc(s["t1_ev"], 1)

            def toe3_evacuate(m):
                act.wait_ge(s["sel_mm"], m + 1)
                v = ps_sel[m % 2][:, 0:G * 11].rearrange("p (g s) -> p g s", g=G)
                for wp in range(2):
                    act.copy(toe3[64 * wp:64 * wp + 64, :, :, m],
                             v[64 * wp:64 * wp + 64, :, wp:wp + SHIFTS]).then_inc(s["sel_ev"], 1)

            def toe4_evacuate(q):
                act.wait_ge(s["sel_mm"], E + q + 1)
                act.copy(toe4[:, :, :, 4 * q:4 * q + 4].rearrange("p g c m -> p m g c"),
                         ps_sel[q % 2][:, :].rearrange("p (m g c) -> p m g c", m=4, g=G)).then_inc(s["sel_ev"], 1)

            act.wait_ge(s["p4_tr"], 1)
            act.copy(p4_rows[0:CI * K4].rearrange("p g c -> p (g c)"),
                     ps_sel[1][0:CI * K4, 0:C]).then_inc(s["p4_ev"], 1)
            for m in range(E):
                toe3_evacuate(m)
                t1_evacuate(m)
            for q in range(4):
                toe4_evacuate(q)
            t1_evacuate(N)
            for g in range(G):
                act.wait_ge(s["conv"], g + 1)
                if g >= 2:
                    act.wait_ge(s["t4_mm"], g - 1)
                act.copy(t3_sb[:, g % 2, :], ps_t3[g % 2]).then_inc(s["t3_ev"], 1)
            act.wait_ge(s["gst"], 1)
            act.activation(rs1[:, 1, :], rs1[:, 0, :], ACT.Sqrt, bias=eps[:, 0:1]).then_inc(s["gst_q"], 1)

            def first_u(k):
                act.wait_ge(s["t5"], k + 1)
                if k >= 2:
                    act.wait_ge(s["t6_mm"], k - 2)
                if k == 0:
                    act.wait_ge(s["rs1"], 1)
                scale = p6_sb[:, 1:2] if k == 0 else a6[:, 1, k - 1:k]
                dst = q6 if k == 0 else u_sb[:, k % 2, :]
                act.activation(dst, ps_t5[:, 0:NF], ACT.Identity, scale=scale).then_inc(s["u_act"], 1)

            act.wait_ge(s["zeros"], 2)
            first_u(0)
            for t in range(N + 2):
                if t < N:
                    first_u(t + 1)
                    if t >= 2:
                        act.wait_ge(s["o_mm"], t - 1)
                    act.activation(g1[:, t % 2, W:W + HW], x_sb[:, t, :], ACT.Identity,
                                   bias=rs1[:, 2, t:t + 1], scale=rs1[:, 1, t:t + 1]).then_inc(s["g1"], 1)
                    act.wait_ge(s["t6_mm"], t + 1)
                    if t >= 2:
                        act.wait_ge(s["o_mm"], t - 1)
                    act.copy(t6t[:, t % 2], ps_t6[:, 0:NF].rearrange("p (k c) -> p k c", k=3)).then_inc(s["t6_ev"], 1)
                n = t - 2
                if n >= 0:
                    z = ps_z[:, 0:J * J].rearrange("p (i j) -> p i j", i=J)
                    act.wait_ge(s["z_mm"], n + 1)
                    if n >= 2:
                        act.wait_ge(s["zh"], n - 1)
                    act.copy(zp[:, n % 2, :, 1:J + 1], z)
                    act.copy(zp[:, n % 2, :, 0:ZP:ZP - 1], z[:, :, 0:J:J - 1])
                    act.mul(z3[:, n % 2], z, 3.0).then_inc(s["z_ev"], 1)
                n = t - 1
                if 0 <= n < N:
                    act.wait_ge(s["st2_v"], n + 1)
                    act.activation(rs2[:, n % 2, 2:3], rs2[:, n % 2, 1:2], ACT.Sqrt,
                                   bias=eps[:, 0:1]).then_inc(s["st2_q"], 1)
                    act.wait_ge(s["st2_r"], n + 1)
                    act.activation(y_sb[:, n, :], x_sb[:, n, :], ACT.Identity, bias=rs2[:, n % 2, 4:5],
                                   scale=rs2[:, n % 2, 3:4]).then_inc(s["g2"], 1)
            act.wait_ge(s["fin_s"], 1)
            act.activation(fin[:, 3:4], fin[:, 2:3], ACT.Sqrt, bias=eps[:, 0:1]).then_inc(s["fin_q"], 1)
            act.wait_ge(s["fin"], 1)
            for n in range(N):
                act.activation(y_sb[:, n, :], y_sb[:, n, :], ACT.Relu, bias=fin[:, 6:7],
                               scale=fin[:, 5:6]).then_inc(s["relu"], 1)

        @block.tensor
        def _(pe):
            pe.wait_ge(s["const"], 1)
            pe.wait_ge(s["p1_in"], 64)
            pe.wait_ge(s["sel"], 2)

            def t1_product(n):
                if n < N:
                    pe.wait_ge(s["xa"], n + 1)
                if n >= 2:
                    pe.wait_ge(s["t1_ev"], n - 1)
                for wp in range(2):
                    rhs = xa[:, n % 2, wp:W:2, :] if n < N else ones_row
                    mm = pe.matmul(ps_t1[n % 2][64 * wp:64 * wp + 64, :], p1_blk, rhs, start=True, stop=True)
                mm.then_inc(s["t1_mm"], 1)

            def toe3_product(m):
                if m >= 2:
                    pe.wait_ge(s["sel_ev"], 2 * (m - 1))
                pe.matmul(ps_sel[m % 2][:, 0:G * 11], sel[0:CI * KD, 0, m].rearrange("p v q -> p (v q)"),
                          p3_rows[0:CI * KD].rearrange("p g s -> p (g s)"), start=True, stop=True).then_inc(s["sel_mm"], 1)

            def toe4_product(q):
                pe.wait_ge(s["sel_ev"], 2 * (E - 1 + q) if q < 2 else 2 * E + q - 1)
                for r in range(4):
                    m = 4 * q + r
                    mm = pe.matmul(ps_sel[q % 2][:, 128 * r:128 * r + 128],
                                   sel[0:CI * K4, 1, m].rearrange("p v q -> p (v q)"),
                                   p4_rows[0:CI * K4].rearrange("p g c -> p (g c)"), start=True, stop=True)
                mm.then_inc(s["sel_mm"], 1)

            pe.wait_ge(s["sel"], 2)
            pe.wait_ge(s["sel_rows"], 16 * (CI + 1))
            pe.transpose(ps_sel[1][0:CI * K4, 0:C], p4_raw, ident[:, :]).then_inc(s["p4_tr"], 1)
            for m in range(E):
                if m == 1:
                    pe.wait_ge(s["p4_ev"], 1)
                toe3_product(m)
                t1_product(m)
            for q in range(4):
                toe4_product(q)
            t1_product(N)
            pe.wait_ge(s["w_pm"], 1)
            pe.wait_ge(s["sel_ev"], 2 * E + 3)
            for k in range(4):
                mm = pe.transpose(ps_sel[0][:, C * k:C * k + C], w_perm[:, k, :], ident[:, :])
            mm.then_inc(s["tr_w"], 1)

            def t4_product(g):
                pe.wait_ge(s["t3_ev"], g + 1)
                if g >= 2:
                    pe.wait_ge(s["t4_ev"], g - 1)
                pe.matmul(ps_t4[g % 2], s4[:, g % 2].rearrange("p v m -> p (v m)"), t3_sb[:, g % 2, :],
                          start=True, stop=True).then_inc(s["t4_mm"], 1)

            pe.wait_ge(s["t1_ev"], NO)
            pe.wait_ge(s["zeros"], 1)
            for g in range(G):
                pe.wait_ge(s["s3"], g + 1)
                if g >= 2:
                    pe.wait_ge(s["t3_ev"], g - 1)
                for t in range(TAPS):
                    mm = pe.matmul(ps_t3[g % 2], s3[:, g % 2, 2 * t:2 * t + 2].rearrange("p s c m -> p (s c m)"),
                                   t1[:, g, t:t + J, :].rearrange("p j n -> p (j n)"),
                                   start=(t == 0), stop=(t == TAPS - 1))
                mm.then_inc(s["conv"], 1)
                if g >= 1:
                    t4_product(g - 1)
            t4_product(G - 1)
            pe.wait_ge(s["st1"], 1)
            pe.matmul(ps_st[:, 0:2 * N], g_mean[:, :, :].rearrange("p a b -> p (a b)"),
                      mv1[:, :, :].rearrange("p n a -> p (n a)"), start=True, stop=True).then_inc(s["gst_mm"], 1)

            def t5_product(k):
                pe.wait_ge(s["dn"], k + 1)
                if k >= 1:
                    pe.wait_ge(s["u"], k)
                for jc in range(JC):
                    mm = pe.matmul(ps_t5[:, 0:NF], dn[:, k % 2, jc, :], p5_sb[:, jc, :],
                                   start=(jc == 0), stop=(jc == JC - 1))
                mm.then_inc(s["t5"], 1)

            t5_product(0)
            for t in range(N + 2):
                if t < N:
                    t5_product(t + 1)
                n = t - 1
                if 0 <= n < N:
                    pe.wait_ge(s["t6_ev"], n + 1)
                    pe.wait_ge(s["g1"], n + 1)
                    for hh in range(2):
                        if n >= 1:
                            pe.wait_ge(s["x1"], 2 * (n - 1) + hh + 1)
                        for k in range(3):
                            lo = (H // 2 * hh + k) * W
                            mm = pe.matmul(ps_o[:, HALF * hh:HALF * hh + HALF], t6t[:, n % 2, k, :],
                                           g1[:, n % 2, lo:lo + HALF], start=(k == 0), stop=(k == 2))
                        if hh:
                            mm.then_inc(s["o_mm"], 1)
                        else:
                            mm.then_inc(s["dve_o0"], 1)
                if t < N:
                    pe.wait_ge(s["u"], t + 2)
                    if t >= 1:
                        pe.wait_ge(s["t6_ev"], t)
                    for k in range(3):
                        v = u_sb[:, (t + 1) % 2, C * k:C * k + C]
                        mm = pe.transpose(ps_t6[:, C * k:C * k + C], v, ident[:, :])
                    mm.then_inc(s["t6_mm"], 1)
                n = t - 2
                if n >= 0:
                    pe.wait_ge(s["g2"], n + 1)
                    if n >= 1:
                        pe.wait_ge(s["z_ev"], n)
                    ph = y_sb[:, n, :].rearrange("p (i a j b) -> p a b i j", a=2, b=2, i=J)
                    for q in range(4):
                        mm = pe.matmul(ps_z[:, 0:J * J], w_t[:, 1 + q, :], ph[:, q // 2, q % 2],
                                       start=(q == 0), stop=(q == 3))
                    mm.then_inc(s["z_mm"], 1)
                    if n >= 1:
                        pe.wait_ge(s["y_rd"], n)
                    for hh in range(2):
                        mm = pe.matmul(ps_y[:, HALF * hh:HALF * hh + HALF], w_t[:, 0, :],
                                       y_sb[:, n, HALF * hh:HALF * hh + HALF], start=True, stop=True)
                    mm.then_inc(s["y_mm"], 1)
                n = t - 1
                if 0 <= n < N:
                    pe.wait_ge(s["st2"], n + 1)
                    if n >= 1:
                        pe.wait_ge(s["st2_v"], n)
                    pe.matmul(ps_st[:, 0:2], g_mean[:, :, :].rearrange("p a b -> p (a b)"), mv2[:, n % 2, :],
                              start=True, stop=True).then_inc(s["st2_mm"], 1)

        @block.vector
        def _(dve):
            link = chained(dve, "dve")
            for n in range(N):
                dve.wait_ge(x_in[n // 2], 16 * CI)
                if n >= 2:
                    dve.wait_ge(s["t1_mm"], n - 1)
                dve.transpose(xa[:, n % 2], x_sb[:, n, :].rearrange("p (h w) -> p w h", w=W)).then_inc(s["xa"], 1)
            dve.wait_ge(s["tr_w"], 1)
            link(dve.tensor_copy(w_t[:, 0, :], ps_sel[0][:, 0:C]))
            link(dve.tensor_scalar(w_det, ps_sel[0][:, C:4 * C].rearrange("p (k c) -> p k c", k=3),
                                   1.0 / 32, None, ALU.mult))
            w1, w2, w3 = (w_det[:, k, :] for k in range(3))
            link(dve.tensor_tensor(w_t[:, 1, :], w2, w3, ALU.add))
            link(dve.tensor_tensor(w_t[:, 3, :], w2, w3, ALU.subtract))
            link(dve.tensor_tensor(w_t[:, 2, :], w1, w_t[:, 1, :], ALU.subtract))
            link(dve.tensor_tensor(w_t[:, 1, :], w1, w_t[:, 1, :], ALU.add))
            link(dve.scalar_tensor_tensor(w_t[:, 4, :], w1, -1.0, w_t[:, 3, :], ALU.mult, ALU.subtract))
            link(dve.scalar_tensor_tensor(w_t[:, 3, :], w_t[:, 3, :], 2.0, w_t[:, 4, :], ALU.mult, ALU.add))
            dve.tensor_copy(gs1[:, 0, :], w_t[:, 0, 0:2]).then_inc(s["w_det"], 1)

            def t4_evacuate(g):
                b = g // GB
                dve.wait_ge(s["t4_mm"], g + 1)
                if b >= 2 and g % GB == 0:
                    dve.wait_ge(d_in[b - 2], 16 * 2 * JL * CI)
                dve.tensor_copy(t4_out[:, b % 2, :, :, g % GB, :].rearrange("p jl jc n -> p jc jl n"),
                                ps_t4[g % 2].rearrange("p (jc jl n) -> p jc jl n", jc=JC, jl=JL)).then_inc(s["t4_ev"], 1)

            for g in range(G):
                t4_evacuate(g)
                if g % 2 == 1:
                    n = g // 2
                    for hh in range(2):
                        ins = dve.bn_stats(st1[:, n, 6 * hh:6 * hh + 6], x_sb[:, n, HALF * hh:HALF * hh + HALF])
                    link(ins)
                    link(dve.bn_aggr(mv1[:, n, :], st1[:, n, :]))
            link(dve.tensor_tensor(rs1[:, 0, :], mv1[:, :, 0], mv1[:, :, 0], ALU.mult))
            dve.tensor_tensor(mv1[:, :, 1], mv1[:, :, 1], rs1[:, 0, :], ALU.add).then_inc(s["st1"], 1)
            dve.wait_ge(s["gst_mm"], 1)
            link(dve.tensor_copy(gs1[:, :, :].rearrange("p n a -> p (n a)"), ps_st[:, 0:2 * N]))
            link(dve.tensor_tensor(rs1[:, 0, :], gs1[:, :, 0], gs1[:, :, 0], ALU.mult))
            link(dve.tensor_tensor(rs1[:, 0, :], gs1[:, :, 1], rs1[:, 0, :], ALU.subtract))
            dve.tensor_scalar(rs1[:, 0, :], rs1[:, 0, :], 0.0, None, ALU.max).then_inc(s["gst"], 1)
            dve.wait_ge(s["gst_q"], 1)
            link(dve.reciprocal(rs1[:, 1, :], rs1[:, 1, :]))
            link(dve.scalar_tensor_tensor(rs1[:, 2, :], gs1[:, :, 0], -1.0, rs1[:, 1, :], ALU.mult, ALU.mult))
            link(dve.tensor_scalar(p6_sb[:, :], p6_sb[:, :], float(NF) ** -0.5, None, ALU.mult))
            for d in range(3):
                last = dve.tensor_scalar(a6[:, d, :], rs1[:, 1, :], p6_sb[:, d:d + 1], None, ALU.mult)
            last.then_inc(s["rs1"], 1)

            def rest_of_u(k):
                dst = q6 if k == 0 else u_sb[:, k % 2, :]
                lo, hi = (p6_sb[:, d:d + 1] if k == 0 else a6[:, d, k - 1:k] for d in (0, 2))
                dve.wait_ge(s["u_act"], k + 1)
                parts = [(C, 2 * C, 0), (G, 3 * G, 2 * C), (1, G - 1, 3 * C - G)]
                for to, n, frm in parts:
                    ins = dve.scalar_tensor_tensor(dst[:, to:to + n], ps_t5[:, frm:frm + n], lo, dst[:, to:to + n],
                                                   ALU.mult, ALU.add)
                link(ins)
                parts = [(0, 2 * C, C), (2 * C, 3 * G, G), (3 * C - G, G - 1, 1)]
                for to, n, frm in parts:
                    ins = dve.scalar_tensor_tensor(dst[:, to:to + n], ps_t5[:, frm:frm + n], hi, dst[:, to:to + n],
                                                   ALU.mult, ALU.add)
                if k == 0:
                    ins.then_inc(s["u"], 1)
                    dve.wait_ge(s["u"], 1)
                else:
                    link(ins)
                    dve.scalar_tensor_tensor(dst, q6, rs1[:, 2, k - 1:k], dst, ALU.mult, ALU.add).then_inc(s["u"], 1)

            rest_of_u(0)
            for t in range(N + 2):
                if t < N:
                    rest_of_u(t + 1)
                n = t - 1
                if 0 <= n < N:
                    b = n % 2
                    for hh in range(2):
                        sl = slice(HALF * hh, HALF * hh + HALF)
                        dve.wait_ge(s["o_mm"] if hh else s["dve_o0"], n + 1)
                        if hh == 0:
                            dve.wait_ge(s["g1"], n + 1)
                        dve.tensor_tensor(x_sb[:, n, sl], x_sb[:, n, sl], ps_o[:, sl], ALU.add).then_inc(s["x1"], 1)
                        dve.wait_ge(s["x1"], 2 * n + hh + 1)
                        ins = dve.bn_stats(st2[:, b, 6 * hh:6 * hh + 6], x_sb[:, n, sl])
                    link(ins)
                    link(dve.bn_aggr(mv2[:, b, :], st2[:, b, :]))
                    dve.scalar_tensor_tensor(mv2[:, b, 1:2], mv2[:, b, 0:1], mv2[:, b, 0:1], mv2[:, b, 1:2],
                                             ALU.mult, ALU.add).then_inc(s["st2"], 1)
                n = t - 2
                if n >= 0:
                    b = n % 2
                    dve.wait_ge(s["zh"], n + 1)
                    dve.wait_ge(s["y_mm"], n + 1)
                    yr = y_sb[:, n, :].rearrange("p (i a w) -> p a i w", a=2, w=W)
                    pr = ps_y[:, :].rearrange("p (i a w) -> p a i w", a=2, w=W)
                    for a in range(2):
                        ins = dve.tensor_tensor(yr[:, a], pr[:, a], zh[:, b, 2 * a:2 * a + J, :], ALU.add)
                        ins.then_inc(s["y_rd"], 1) if a else None
                    dve.wait_ge(s["y_rd"], n + 1)
                    for a in range(2):
                        ins = dve.scalar_tensor_tensor(yr[:, a], zh[:, b, 1:J + 1, :], 3.0, yr[:, a], ALU.mult, ALU.add)
                    ins.then_inc(s["y"], 1)
                    dve.wait_ge(s["y"], n + 1)
                    for hh in range(2):
                        dve.bn_stats(sty[:, n, 6 * hh:6 * hh + 6], y_sb[:, n, HALF * hh:HALF * hh + HALF]).then_inc(s["sty"], 1)
                n = t - 1
                if 0 <= n < N:
                    b = n % 2
                    dve.wait_ge(s["st2_mm"], n + 1)
                    link(dve.tensor_copy(gs2[:, b, :], ps_st[:, 0:2]))
                    link(dve.tensor_tensor(rs2[:, b, 0:1], gs2[:, b, 0:1], gs2[:, b, 0:1], ALU.mult))
                    link(dve.tensor_tensor(rs2[:, b, 1:2], gs2[:, b, 1:2], rs2[:, b, 0:1], ALU.subtract))
                    dve.tensor_scalar(rs2[:, b, 1:2], rs2[:, b, 1:2], 0.0, None, ALU.max).then_inc(s["st2_v"], 1)
                    dve.wait_ge(s["st2_q"], n + 1)
                    link(dve.reciprocal(rs2[:, b, 3:4], rs2[:, b, 2:3]))
                    dve.scalar_tensor_tensor(rs2[:, b, 4:5], gs2[:, b, 0:1], -1.0, rs2[:, b, 3:4],
                                             ALU.mult, ALU.mult).then_inc(s["st2_r"], 1)
            dve.wait_ge(s["sty"], 2 * N)
            link(dve.bn_aggr(fin[:, 1:3], sty[:, :, :].rearrange("p n a -> p (n a)")))
            dve.tensor_scalar(fin[:, 2:3], fin[:, 2:3], 0.0, None, ALU.max).then_inc(s["fin_s"], 1)
            dve.wait_ge(s["fin_q"], 1)
            link(dve.reciprocal(fin[:, 4:5], fin[:, 3:4]))
            link(dve.tensor_tensor(fin[:, 5:6], fin[:, 4:5], gb[:, 0:1], ALU.mult))
            link(dve.tensor_tensor(fin[:, 7:8], fin[:, 1:2], fin[:, 5:6], ALU.mult))
            dve.tensor_tensor(fin[:, 6:7], gb[:, 1:2], fin[:, 7:8], ALU.subtract).then_inc(s["fin"], 1)
            for n in range(N):
                dve.wait_ge(s["relu"], n + 1)
                dve.tensor_tensor(x_sb[:, n, :], x_sb[:, n, :], y_sb[:, n, :], ALU.add).then_inc(s["res"], 1)


INPUTS = {"x": "x", "p1": "L0_conv_p1", "p3": "L0_conv_p3", "p4": "L0_conv_p4", "p5": "L0_conv_p5",
          "p6": "L0_conv_p6", "conv_w": "L1_conv_conv_w", "gamma": "L1_conv_gamma", "beta": "L1_conv_beta"}


def kernel(x, L0_conv_p1, L0_conv_p3, L0_conv_p4, L0_conv_p5, L0_conv_p6, L1_conv_conv_w, L1_conv_gamma,
           L1_conv_beta):
    import numpy as np
    import concourse.bacc as bacc
    from concourse.bass_utils import run_bass_kernel_spmd

    given = [x, L0_conv_p1, L0_conv_p3, L0_conv_p4, L0_conv_p5, L0_conv_p6, L1_conv_conv_w, L1_conv_gamma,
             L1_conv_beta]
    nc = bacc.Bacc("TRN2", target_bir_lowering=False, num_devices=1)
    arrays = {"in_" + k: np.ascontiguousarray(v) for k, v in zip(INPUTS, given)}
    args = [nc.dram_tensor(k, v.shape, mybir.dt.from_np(v.dtype), kind="ExternalInput").ap()
            for k, v in arrays.items()]
    out = nc.dram_tensor("out", (N, C, H, W), F32, kind="ExternalOutput").ap()
    build(nc, *args, out)
    result = run_bass_kernel_spmd(nc, [arrays], core_ids=[0])
    return result.results[0]["out"]
```

```python
import concourse.bass as bass
from concourse import mybir
from contextlib import ExitStack

F32 = mybir.dt.float32
F32R = mybir.dt.float32r
ALU = mybir.AluOpType
ACT = mybir.ActivationFunctionType

N, C, H, W = 16, 128, 32, 32
HW = H * W
CI = 4
G = C // CI
E = 16
KD, KX = 9, 9
K4 = 5
NF = 3 * C
J = W // 2
JP = J + 4
NO = N + 1
TAPS = 5
SHIFTS = 2 * TAPS
NB, GB = 4, 8
JC, JL = 4, 4
GN_EPS = 1e-5
BN_EPS = 1e-5
HALF = HW // 2
ZP = J + 2
XR = 3


def build(nc, x, p1, p3, p4, p5, p6, conv_w, gamma, beta, out):
    ctx = ExitStack()
    with ctx:
        def sem(name):
            return ctx.enter_context(nc.semaphore(name))

        base = -(-nc.sbuf_base // 32) * 32
        whole = ctx.enter_context(nc.sbuf_tensor("whole", [128, (nc.sbuf_top - base) // 4 - 8], F32))
        cursor = [base]

        def put(name, shape, dtype=F32):
            t = nc.alloc_sbuf_tensor_at(name, [128] + list(shape), dtype, offset=cursor[0])
            n = 4
            for k in shape:
                n *= k
            cursor[0] += -(-n // 32) * 32
            return t

        ident = put("ident", [128])
        g_mean = put("g_mean", [CI, G])
        ci_mask = put("ci_mask", [CI])
        v_mask = put("v_mask", [2])
        p6_sb = put("p6_sb", [3])
        a6 = put("a6", [3, N])
        gb = put("gb", [2])
        sty = put("sty", [N, 12])
        st1 = sty
        mv1 = put("mv1", [N, 2])
        gs1 = put("gs1", [N, 2])
        rs1 = put("rs1", [3, N])
        st2 = put("st2", [2, 12])
        mv2 = put("mv2", [2, 2])
        gs2 = put("gs2", [2, 2])
        rs2 = put("rs2", [2, 5])
        fin = put("fin", [8])
        eps = put("eps", [1])
        p5_sb = put("p5_sb", [JC, NF])
        w_hi = put("w_hi", [5, C], F32R)
        w_lo = put("w_lo", [5, C], F32R)

        region_d = cursor[0]
        x_ring = put("x_ring", [XR, 2, HW])
        xa = put("xa", [2, W, G])
        p4_raw = put("p4_raw", [CI * K4])
        p4_hi = put("p4_hi", [C], F32R)
        p4_lo = put("p4_lo", [C], F32R)
        p1_blk = put("p1_blk", [CI * E])
        mask8 = put("mask8", [8])
        in_d = cursor[0]
        cursor[0] = region_d
        d_sb = put("d_sb", [JC, C, NO])
        region_s = cursor[0]
        assert in_d <= region_s

        t1_hi = put("t1_hi", [G, JP, NO], F32R)
        t1_lo = put("t1_lo", [G, JP, NO], F32R)
        toe3 = put("toe3", [G, SHIFTS, E])
        at_toe4 = cursor[0]
        toe4 = put("toe4", [G, CI, E])
        at_s3 = cursor[0]
        s3_f = put("s3_f", [2, SHIFTS, CI, E])
        s3_hi = put("s3_hi", [2, SHIFTS * CI * E], F32R)
        s3_lo = put("s3_lo", [2, SHIFTS * CI * E], F32R)
        s4_f = put("s4_f", [4, 2, CI * E])
        s4_hi = put("s4_hi", [4, 128], F32R)
        s4_lo = put("s4_lo", [4, 128], F32R)
        at_t3 = cursor[0]
        t3_hi = put("t3_hi", [2, J * NO], F32R)
        t3_lo = put("t3_lo", [2, J * NO], F32R)
        at_t4 = cursor[0]
        t4_out = put("t4_out", [2, JL, JC, GB, NO])
        p3_rows = put("p3_rows", [G * 11])
        p3_hi = put("p3_hi", [G * 11], F32R)
        p3_lo = put("p3_lo", [G * 11], F32R)
        assert cursor[0] <= nc.sbuf_top
        cursor[0] = at_toe4
        sel_half = put("sel_half", [2, E, CI, E])
        assert cursor[0] <= at_s3
        cursor[0] = at_s3
        p5_raw = put("p5_raw", [JC, NF])
        w_raw = put("w_raw", [4 * C])
        w_perm = put("w_perm", [4, C])
        w_det = put("w_det", [3, C])
        w_f = put("w_f", [5, C])
        assert cursor[0] <= at_t3
        cursor[0] = at_t3
        ones_row = put("ones_row", [HALF])
        cursor[0] = at_t4
        sel = put("sel", [2, E, 2, CI * E], F32R)

        cursor[0] = region_s
        x_sb = put("x_sb", [N, HW])
        y_sb = put("y_sb", [N, HW])
        g1_hi = put("g1_hi", [(H + 2) * W], F32R)
        g1_lo = put("g1_lo", [(H + 2) * W], F32R)
        g2_hi = put("g2_hi", [HW], F32R)
        g2_lo = put("g2_lo", [HW], F32R)
        t6_hi = put("t6_hi", [3, C], F32R)
        t6_lo = put("t6_lo", [3, C], F32R)
        u_sb = put("u_sb", [2, NF])
        q6 = put("q6", [NF])
        zp = put("zp", [J, ZP])
        z3 = put("z3", [2, J, J])
        zh = put("zh", [2, ZP, W])
        assert cursor[0] <= nc.sbuf_top

        bank = [ctx.enter_context(nc.psum_tensor(f"bank{i}", [128, 512], F32)) for i in range(4)]
        wide = [ctx.enter_context(nc.psum_tensor(f"wide{i}", [128, 1024], F32)) for i in range(2)]
        ps_t1 = [bank[0], bank[1]]
        ps_sel = [bank[2], bank[3]]
        ps_t3 = [wide[0][:, 0:J * NO], wide[0][:, 512:512 + J * NO]]
        ps_t4 = [wide[1][:, 0:J * NO], wide[1][:, 512:512 + J * NO]]
        ps_t5, ps_t6, ps_z, ps_st = bank
        ps_o, ps_y = wide

        names = ("const zeros sel sel_rows w_in p1_in xa x_used t1_mm t1_hi t1_lo p3_hi p3_lo p4_tr p4_hi p4_lo "
                 "sel_mm sel_ev w_pm p5_pm w_tr w_f w_hi w_lo s_f s_hi s_lo conv t3_hi t3_lo t4_mm t4_ev "
                 "st1 gst_mm gst gst_q rs1 t5 u_act u t6_mm t6_hi t6_lo g1_f g1_hi g1_lo o_half o_mm x1 "
                 "st2 st2_mm st2_v st2_q st2_r g2_f g2_hi g2_lo z_mm z_ev zh y_mm y_rd y sty "
                 "fin_s fin_q fin relu res dve pool act stored").split()
        s = {n: sem("s_" + n) for n in names}
        x_in = [sem(f"s_x_in{k}") for k in range(N // 2)]
        d_in = [sem(f"s_d_in{b}") for b in range(NB)]

        def chained(eng, name):
            count = [0]

            def link(ins):
                count[0] += 1
                ins.then_inc(s[name], 1)
                eng.wait_ge(s[name], count[0])
            return link

        def split_product(ps, w, m, start, stop):
            nc.tensor.matmul(ps, w[0], m[0], start=start, stop=False)
            nc.tensor.matmul(ps, w[0], m[1], start=False, stop=False)
            return nc.tensor.matmul(ps, w[1], m[0], start=False, stop=stop)

        block = ctx.enter_context(nc.Block())

        def load_x(eng, dst, k):
            for ci in range(CI):
                eng.dma_start(dst[G * ci:G * ci + G],
                              x[2 * k:2 * k + 2].rearrange("n (g c) h w -> c g n (h w)", c=CI)[ci]
                              ).then_inc(x_in[k], 16)

        @block.sync
        def _(sp):
            sp.wait_ge(s["zeros"], 1)
            for ci in range(CI):
                sp.dma_start(p3_rows[KD * ci:KD * ci + KD, :].rearrange("p (g s) -> p g s", g=G)[:, :, 1:1 + KX],
                             p3.rearrange("(g c) o y x -> c y g (o x)", c=CI)[ci]).then_inc(s["sel_rows"], 16)
            sp.dma_start(p4_raw[:, :], p4.rearrange("c i y x -> c (i y x)")).then_inc(s["sel_rows"], 16)
            for ci in range(CI):
                sp.dma_start(p1_blk[32 * ci:32 * ci + 32, E * ci:E * ci + E], p1).then_inc(s["p1_in"], 16)
            for k in range(N // 2):
                if k >= XR:
                    sp.wait_ge(s["x_used"], 2 * (k - XR + 1))
                load_x(sp, x_ring[:, k % XR], k)
            for ci in range(CI):
                q = slice(G * ci, G * ci + G)
                sp.dma_start(w_raw[q, :], conv_w.rearrange("(g c) f -> c g f", c=CI)[ci]).then_inc(s["w_in"], 16)
                sp.dma_start(p6_sb[q, :], p6.rearrange("(g c) a b d -> c g (a b d)", c=CI)[ci]).then_inc(s["w_in"], 16)
                sp.dma_start(gb[q, 0:1], gamma.rearrange("(g c a) -> c g a", c=CI, a=1)[ci],
                             allow_slow_non_contiguous=True).then_inc(s["w_in"], 16)
                sp.dma_start(gb[q, 1:2], beta.rearrange("(g c a) -> c g a", c=CI, a=1)[ci],
                             allow_slow_non_contiguous=True).then_inc(s["w_in"], 16)
            for jl in range(JL):
                for v in range(2):
                    sp.dma_start(p5_raw[32 * jl + 16 * v:32 * jl + 16 * v + 16, :, :],
                                 p5.rearrange("e (j r) o f -> r e j (o f)", r=2 * JL)[2 * jl + 1 - v]
                                 ).then_inc(s["w_in"], 16)
            for b in range(NB):
                sp.wait_ge(s["t4_ev"], GB * (b + 1))
                if b == 0:
                    sp.wait_ge(s["t1_mm"], NO)
                    sp.wait_ge(s["x_used"], N)
                for jl in range(JL):
                    for v in range(2):
                        for co in range(CI):
                            src, dst = 64 * v + E * co, 32 * jl + E * v
                            sp.dma_start(
                                d_sb[dst:dst + E, :, G * co + GB * b:G * co + GB * b + GB, :].rearrange(
                                    "p j g n -> p j (g n)"),
                                t4_out[src:src + E, b % 2, jl].rearrange("p j g n -> p j (g n)")
                                ).then_inc(d_in[b], 16)
            sp.wait_ge(s["conv"], G)
            for k in range(N // 2):
                load_x(sp, x_sb[:, 2 * k:2 * k + 2, :], k)
            for n in range(0, N, 2):
                sp.wait_ge(s["res"], n + 2)
                for ci in range(CI):
                    sp.dma_start(out[n:n + 2].rearrange("n (g c) h w -> c g n (h w)", c=CI)[ci],
                                 x_sb[G * ci:G * ci + G, n:n + 2, :]).then_inc(s["stored"], 16)
            sp.wait_ge(s["stored"], 16 * CI * N // 2)

        @block.gpsimd
        def _(pool):
            link = chained(pool, "pool")
            pool.memset(p1_blk[:, :], 0.0)
            pool.memset(p3_rows[:, :], 0.0).then_inc(s["zeros"], 1)
            pool.memset(ident[:, :], 0.0)
            pool.memset(mask8[:, :], 1.0)
            pool.memset(v_mask[:, :], 1.0)
            pool.memset(eps[:, :], GN_EPS)
            link(pool.memset(sel_half[:, :, :, :, :], 0.0))
            pool.affine_select(out=ident[:, :], in_=ident[:, :], compare_op=ALU.not_equal, fill=1.0,
                               base=0, pattern=[[-1, 128]], channel_multiplier=1).then_inc(s["const"], 1)
            for i, (k, half) in enumerate(((KD, KD // 2), (K4, K4 // 2))):
                v = sel_half[0:CI * k, i]
                link(pool.affine_select(out=v, in_=v, compare_op=ALU.not_equal, fill=1.0, base=-half,
                                        pattern=[[1, E], [-k, CI], [-1, E]], channel_multiplier=1))
                link(pool.affine_select(out=v, in_=v, compare_op=ALU.is_ge, fill=0.0, base=half,
                                        pattern=[[-1, E], [0, CI], [1, E]], channel_multiplier=0))
                link(pool.affine_select(out=v, in_=v, compare_op=ALU.is_ge, fill=0.0, base=k - 1 - half,
                                        pattern=[[1, E], [0, CI], [-1, E]], channel_multiplier=0))
                src = v.rearrange("p m c e -> p m (c e)").unsqueeze(2).broadcast_to([CI * k, E, 2, CI * E])
                pool.tensor_copy(sel[0:CI * k, i], src).then_inc(s["sel"], 1)
            for t in (t1_hi, t1_lo):
                pool.memset(t[:, :, 0:2, :].bitcast(F32), 0.0)
                pool.memset(t[:, :, JP - 2:JP, :].bitcast(F32), 0.0).then_inc(s["zeros"], 1)
            pool.memset(ones_row[:, :], 1.0).then_inc(s["const"], 1)
            link(pool.memset(g_mean[:, :, :], 0.0))
            for m in range(CI):
                link(pool.affine_select(out=g_mean[:, :, :], in_=g_mean[:, :, :], compare_op=ALU.not_equal,
                                        fill=1.0 / CI, base=-G * m, pattern=[[0, CI], [-1, G]],
                                        channel_multiplier=1))
            link(pool.affine_select(out=mask8[:, :], in_=mask8[:, :], compare_op=ALU.is_ge, fill=0.0, base=0,
                                    pattern=[[-16, 8]], channel_multiplier=1))
            link(pool.affine_select(out=mask8[:, :], in_=mask8[:, :], compare_op=ALU.is_ge, fill=0.0, base=15,
                                    pattern=[[16, 8]], channel_multiplier=-1))
            link(pool.tensor_tensor(ci_mask[:, :], mask8[:, 0:4], mask8[:, 4:8], ALU.add))
            link(pool.affine_select(out=v_mask[:, :], in_=v_mask[:, :], compare_op=ALU.is_ge, fill=0.0, base=63,
                                    pattern=[[128, 2]], channel_multiplier=-1))
            link(pool.affine_select(out=v_mask[:, :], in_=v_mask[:, :], compare_op=ALU.is_ge, fill=0.0, base=64,
                                    pattern=[[-128, 2]], channel_multiplier=1))
            pool.wait_ge(s["w_in"], 16 * 24)
            pool.tensor_copy(w_perm[:, :, :].rearrange("p k (c g) -> p k c g", c=CI),
                             w_raw[:, :].rearrange("p (k g c) -> p k c g", k=4, c=CI)).then_inc(s["w_pm"], 1)
            for jc in range(JC):
                last = pool.tensor_copy(p5_sb[:, jc, :].rearrange("p (k c g) -> p k c g", k=3, c=CI),
                                        p5_raw[:, jc, :].rearrange("p (g c k) -> p k c g", c=CI, k=3))
            last.then_inc(s["p5_pm"], 1)
            pool.wait_ge(s["p5_pm"], 1)
            pool.wait_ge(s["w_lo"], 1)
            pool.wait_ge(s["sel_ev"], 36)
            for g in range(G):
                if g >= 2:
                    pool.wait_ge(s["s_lo"], g - 1)
                pool.tensor_tensor(
                    s3_f[:, g % 2], toe3[:, g].unsqueeze(2).broadcast_to([128, SHIFTS, CI, E]),
                    ci_mask[:, :].unsqueeze(1).unsqueeze(3).broadcast_to([128, SHIFTS, CI, E]), ALU.mult)
                pool.tensor_tensor(
                    s4_f[:, g % 4], toe4[:, g].rearrange("p c m -> p (c m)").unsqueeze(1).broadcast_to([128, 2, CI * E]),
                    v_mask[:, :].unsqueeze(2).broadcast_to([128, 2, CI * E]), ALU.mult).then_inc(s["s_f"], 1)
            pool.wait_ge(s["t4_mm"], G)
            for b in range(NB):
                pool.wait_ge(d_in[b], 16 * 2 * JL * CI)
            for t in (g1_hi, g1_lo):
                v = t[:, :].bitcast(F32).rearrange("p (i w) -> p i w", w=W)
                pool.memset(v[:, 0:H + 2:H + 1, :], 0.0).then_inc(s["zeros"], 1)
            for t in range(N + 2):
                if t < N:
                    pool.wait_ge(s["g1_hi"], t + 1)
                    pool.tensor_tensor(g1_lo[:, W:W + HW], y_sb[:, t, :], g1_hi[:, W:W + HW].bitcast(F32),
                                       ALU.subtract).then_inc(s["g1_lo"], 1)
                n = t - 2
                if n >= 0:
                    pool.wait_ge(s["z_ev"], n + 1)
                    if n >= 2:
                        pool.wait_ge(s["y"], n - 1)
                    rows = zh[:, n % 2, 1:J + 1, :].rearrange("p i (j a) -> p i j a", a=2)
                    pool.tensor_tensor(rows[:, :, :, 0], z3[:, n % 2], zp[:, :, 0:J], ALU.add)
                    link(pool.tensor_tensor(rows[:, :, :, 1], z3[:, n % 2], zp[:, :, 2:ZP], ALU.add))
                    pool.tensor_copy(zh[:, n % 2, 0:ZP:ZP - 1, :],
                                     zh[:, n % 2, 1:J + 1:J - 1, :]).then_inc(s["zh"], 1)
                n = t - 1
                if 0 <= n < N:
                    pool.wait_ge(s["g2_hi"], n + 1)
                    pool.tensor_tensor(g2_lo[:, :], y_sb[:, n, :], g2_hi[:, :].bitcast(F32),
                                       ALU.subtract).then_inc(s["g2_lo"], 1)

        @block.scalar
        def _(act):
            def t1_high(n):
                act.wait_ge(s["t1_mm"], n + 1)
                act.copy(t1_hi[:, :, 2:2 + J, n].rearrange("p g j -> p j g"),
                         ps_t1[n % 2][:, :].rearrange("p (j g) -> p j g", g=G)).then_inc(s["t1_hi"], 1)

            def toe3_evacuate(m):
                act.wait_ge(s["sel_mm"], m + 1)
                v = ps_sel[m % 2][:, 0:G * 11].rearrange("p (g s) -> p g s", g=G)
                for wp in range(2):
                    act.copy(toe3[64 * wp:64 * wp + 64, :, :, m],
                             v[64 * wp:64 * wp + 64, :, wp:wp + SHIFTS]).then_inc(s["sel_ev"], 1)

            def toe4_evacuate(q):
                act.wait_ge(s["sel_mm"], E + q + 1)
                act.copy(toe4[:, :, :, 4 * q:4 * q + 4].rearrange("p g c m -> p m g c"),
                         ps_sel[q % 2][:, :].rearrange("p (m g c) -> p m g c", m=4, g=G)).then_inc(s["sel_ev"], 1)

            act.wait_ge(s["sel_rows"], 16 * (CI + 1))
            act.copy(p3_hi[0:CI * KD, :], p3_rows[0:CI * KD, :]).then_inc(s["p3_hi"], 1)
            act.wait_ge(s["p4_tr"], 1)
            act.copy(p4_hi[0:CI * K4, :], ps_sel[1][0:CI * K4, 0:C]).then_inc(s["p4_hi"], 1)
            for m in range(E):
                toe3_evacuate(m)
                if m % 4 == 3:
                    t1_high(m // 4)
            for q in range(4):
                toe4_evacuate(q)
                t1_high(4 + q)
            for n in range(8, N):
                t1_high(n)
            t1_high(N)
            act.wait_ge(s["w_f"], 1)
            act.copy(w_hi[:, :, :], w_f[:, :, :]).then_inc(s["w_hi"], 1)

            def split_high(g):
                act.wait_ge(s["s_f"], g + 1)
                if g >= 2:
                    act.wait_ge(s["conv"], g - 1)
                if g >= 4:
                    act.wait_ge(s["t4_mm"], g - 3)
                act.copy(s3_hi[:, g % 2, :], s3_f[:, g % 2].rearrange("p s c m -> p (s c m)"))
                act.copy(s4_hi[:, g % 4, :], s4_f[:, g % 4].rearrange("p v m -> p (v m)")).then_inc(s["s_hi"], 1)

            def t4_evacuate(g):
                b = g // GB
                act.wait_ge(s["t4_mm"], g + 1)
                if b >= 2 and g % GB == 0:
                    act.wait_ge(d_in[b - 2], 16 * 2 * JL * CI)
                act.copy(t4_out[:, b % 2, :, :, g % GB, :].rearrange("p jl jc n -> p jc jl n"),
                         ps_t4[g % 2].rearrange("p (jc jl n) -> p jc jl n", jc=JC, jl=JL)).then_inc(s["t4_ev"], 1)

            split_high(0)
            for g in range(G):
                if g + 1 < G:
                    split_high(g + 1)
                act.wait_ge(s["conv"], g + 1)
                if g >= 2:
                    act.wait_ge(s["t4_mm"], g - 1)
                act.copy(t3_hi[:, g % 2, :], ps_t3[g % 2]).then_inc(s["t3_hi"], 1)
                if g >= 1:
                    t4_evacuate(g - 1)
            t4_evacuate(G - 1)
            act.wait_ge(s["gst"], 1)
            act.activation(rs1[:, 1, :], rs1[:, 0, :], ACT.Sqrt, bias=eps[:, 0:1]).then_inc(s["gst_q"], 1)

            def middle_of_u(k):
                act.wait_ge(s["t5"], k + 1)
                if k >= 3:
                    act.wait_ge(s["t6_mm"], k - 2)
                if k == 0:
                    act.wait_ge(s["rs1"], 1)
                scale = p6_sb[:, 1:2] if k == 0 else a6[:, 1, k - 1:k]
                dst = q6[:, :] if k == 0 else u_sb[:, k % 2, :]
                act.activation(dst, ps_t5[:, 0:NF], ACT.Identity, scale=scale).then_inc(s["u_act"], 1)

            act.wait_ge(s["zeros"], 5)
            middle_of_u(0)
            for t in range(N + 2):
                if t < N:
                    middle_of_u(t + 1)
                    act.wait_ge(x_in[t // 2], 2 * 16 * CI)
                    act.activation(y_sb[:, t, :], x_sb[:, t, :], ACT.Identity, bias=rs1[:, 2, t:t + 1],
                                   scale=rs1[:, 1, t:t + 1]).then_inc(s["g1_f"], 1)
                    act.wait_ge(s["g1_f"], t + 1)
                    if t >= 1:
                        act.wait_ge(s["o_mm"], t)
                    act.copy(g1_hi[:, W:W + HW], y_sb[:, t, :]).then_inc(s["g1_hi"], 1)
                n = t - 2
                if n >= 0:
                    z = ps_z[:, 0:J * J].rearrange("p (i j) -> p i j", i=J)
                    act.wait_ge(s["z_mm"], n + 1)
                    if n >= 1:
                        act.wait_ge(s["zh"], n)
                    act.copy(zp[:, :, 1:J + 1], z)
                    act.copy(zp[:, :, 0:ZP:ZP - 1], z[:, :, 0:J:J - 1])
                    act.mul(z3[:, n % 2], z, 3.0).then_inc(s["z_ev"], 1)
                n = t - 1
                if 0 <= n < N:
                    act.wait_ge(s["st2_v"], n + 1)
                    act.activation(rs2[:, n % 2, 2:3], rs2[:, n % 2, 1:2], ACT.Sqrt,
                                   bias=eps[:, 0:1]).then_inc(s["st2_q"], 1)
                if t < N:
                    act.wait_ge(s["t6_mm"], t + 1)
                    if t >= 1:
                        act.wait_ge(s["o_mm"], t)
                    act.copy(t6_hi[:, :, :], ps_t6[:, 0:NF].rearrange("p (k c) -> p k c", k=3)).then_inc(s["t6_hi"], 1)
                if 0 <= n < N:
                    act.wait_ge(s["st2_r"], n + 1)
                    act.wait_ge(s["g1_lo"], n + 1)
                    act.activation(y_sb[:, n, :], x_sb[:, n, :], ACT.Identity, bias=rs2[:, n % 2, 4:5],
                                   scale=rs2[:, n % 2, 3:4]).then_inc(s["g2_f"], 1)
                    act.wait_ge(s["g2_f"], n + 1)
                    if n >= 1:
                        act.wait_ge(s["y_mm"], n)
                    act.copy(g2_hi[:, :], y_sb[:, n, :]).then_inc(s["g2_hi"], 1)
            act.wait_ge(s["fin_s"], 1)
            act.activation(fin[:, 3:4], fin[:, 2:3], ACT.Sqrt, bias=eps[:, 0:1]).then_inc(s["fin_q"], 1)
            act.wait_ge(s["fin"], 1)
            for n in range(N):
                act.activation(y_sb[:, n, :], y_sb[:, n, :], ACT.Relu, bias=fin[:, 6:7],
                               scale=fin[:, 5:6]).then_inc(s["relu"], 1)

        @block.tensor
        def _(pe):
            def t1_product(n):
                if n < N:
                    pe.wait_ge(s["xa"], n + 1)
                if n >= 2:
                    pe.wait_ge(s["t1_lo"], n - 1)
                for wp in range(2):
                    rhs = xa[:, n % 2, wp:W:2, :] if n < N else ones_row[:, :]
                    mm = pe.matmul(ps_t1[n % 2][64 * wp:64 * wp + 64, :], p1_blk[:, :], rhs, start=True, stop=True)
                mm.then_inc(s["t1_mm"], 1)

            def toe3_product(m):
                if m >= 2:
                    pe.wait_ge(s["sel_ev"], 2 * (m - 1))
                w = sel[0:CI * KD, 0, m].rearrange("p v q -> p (v q)")
                pe.matmul(ps_sel[m % 2][:, 0:G * 11], w, p3_hi[0:CI * KD, :], start=True, stop=False)
                pe.matmul(ps_sel[m % 2][:, 0:G * 11], w, p3_lo[0:CI * KD, :], start=False, stop=True
                          ).then_inc(s["sel_mm"], 1)

            def toe4_product(q):
                pe.wait_ge(s["sel_ev"], 2 * (E - 1 + q) if q < 2 else 2 * E + q - 1)
                for r in range(4):
                    w = sel[0:CI * K4, 1, 4 * q + r].rearrange("p v q -> p (v q)")
                    ps = ps_sel[q % 2][:, 128 * r:128 * r + 128]
                    pe.matmul(ps, w, p4_hi[0:CI * K4, :], start=True, stop=False)
                    mm = pe.matmul(ps, w, p4_lo[0:CI * K4, :], start=False, stop=True)
                mm.then_inc(s["sel_mm"], 1)

            pe.wait_ge(s["const"], 1)
            pe.wait_ge(s["sel_rows"], 16 * (CI + 1))
            pe.transpose(ps_sel[1][0:CI * K4, 0:C], p4_raw[:, :], ident[:, :]).then_inc(s["p4_tr"], 1)
            pe.wait_ge(s["sel"], 2)
            pe.wait_ge(s["p3_lo"], 1)
            pe.wait_ge(s["p1_in"], 64)
            for m in range(E):
                if m == 1:
                    pe.wait_ge(s["p4_lo"], 1)
                toe3_product(m)
                if m % 4 == 3:
                    t1_product(m // 4)
            for q in range(4):
                toe4_product(q)
                t1_product(4 + q)
            for n in range(8, N):
                t1_product(n)
            pe.wait_ge(s["const"], 2)
            t1_product(N)
            pe.wait_ge(s["w_pm"], 1)
            pe.wait_ge(s["sel_ev"], 2 * E + 3)
            for k in range(4):
                mm = pe.transpose(ps_sel[0][:, C * k:C * k + C], w_perm[:, k, :], ident[:, :])
            mm.then_inc(s["w_tr"], 1)

            def t4_product(g):
                pe.wait_ge(s["t3_lo"], g + 1)
                if g >= 2:
                    pe.wait_ge(s["t4_ev"], g - 1)
                split_product(ps_t4[g % 2], (s4_hi[:, g % 4, :], s4_lo[:, g % 4, :]),
                              (t3_hi[:, g % 2, :], t3_lo[:, g % 2, :]), True, True).then_inc(s["t4_mm"], 1)

            pe.wait_ge(s["t1_lo"], NO)
            pe.wait_ge(s["zeros"], 3)
            for g in range(G):
                pe.wait_ge(s["s_lo"], g + 1)
                if g >= 2:
                    pe.wait_ge(s["t3_lo"], g - 1)
                for t in range(TAPS):
                    q = slice(128 * t, 128 * t + 128)
                    mm = split_product(ps_t3[g % 2], (s3_hi[:, g % 2, q], s3_lo[:, g % 2, q]),
                                       [h[:, g, t:t + J, :].rearrange("p j n -> p (j n)") for h in (t1_hi, t1_lo)],
                                       t == 0, t == TAPS - 1)
                mm.then_inc(s["conv"], 1)
                if g >= 1:
                    t4_product(g - 1)
            t4_product(G - 1)
            pe.wait_ge(s["st1"], 1)
            pe.matmul(ps_st[:, 0:2 * N], g_mean[:, :, :].rearrange("p a b -> p (a b)"),
                      mv1[:, :, :].rearrange("p n a -> p (n a)"), start=True, stop=True).then_inc(s["gst_mm"], 1)

            def t5_product(k):
                if k >= 1:
                    pe.wait_ge(s["u"], k)
                for jc in range(JC):
                    mm = pe.matmul(ps_t5[:, 0:NF], d_sb[:, jc, :, (k - 1) % NO], p5_sb[:, jc, :],
                                   start=(jc == 0), stop=(jc == JC - 1))
                mm.then_inc(s["t5"], 1)

            for b in range(NB):
                pe.wait_ge(d_in[b], 16 * 2 * JL * CI)
            t5_product(0)
            for t in range(N + 2):
                if t < N:
                    t5_product(t + 1)
                n = t - 1
                if 0 <= n < N:
                    pe.wait_ge(s["t6_lo"], n + 1)
                    pe.wait_ge(s["g1_lo"], n + 1)
                    for hh in range(2):
                        if n >= 1:
                            pe.wait_ge(s["x1"], 2 * (n - 1) + hh + 1)
                        for k in range(3):
                            lo = (H // 2 * hh + k) * W
                            mm = split_product(ps_o[:, HALF * hh:HALF * hh + HALF], (t6_hi[:, k, :], t6_lo[:, k, :]),
                                               (g1_hi[:, lo:lo + HALF], g1_lo[:, lo:lo + HALF]), k == 0, k == 2)
                        mm.then_inc(s["o_mm"] if hh else s["o_half"], 1)
                n = t - 2
                if n >= 0:
                    pe.wait_ge(s["g2_lo"], n + 1)
                    if n >= 1:
                        pe.wait_ge(s["z_ev"], n)
                    ph = [h[:, :].rearrange("p (i a j b) -> p a b i j", a=2, b=2, i=J) for h in (g2_hi, g2_lo)]
                    for q in range(4):
                        mm = split_product(ps_z[:, 0:J * J], (w_hi[:, 1 + q, :], w_lo[:, 1 + q, :]),
                                           [h[:, q // 2, q % 2] for h in ph], q == 0, q == 3)
                    mm.then_inc(s["z_mm"], 1)
                    if n >= 1:
                        pe.wait_ge(s["y_rd"], n)
                    for hh in range(2):
                        q = slice(HALF * hh, HALF * hh + HALF)
                        mm = split_product(ps_y[:, q], (w_hi[:, 0, :], w_lo[:, 0, :]), (g2_hi[:, q], g2_lo[:, q]),
                                           True, True)
                    mm.then_inc(s["y_mm"], 1)
                n = t - 1
                if 0 <= n < N:
                    pe.wait_ge(s["st2"], n + 1)
                    if n >= 1:
                        pe.wait_ge(s["st2_v"], n)
                    pe.matmul(ps_st[:, 0:2], g_mean[:, :, :].rearrange("p a b -> p (a b)"), mv2[:, n % 2, :],
                              start=True, stop=True).then_inc(s["st2_mm"], 1)
                if t < N:
                    pe.wait_ge(s["u"], t + 2)
                    if t >= 1:
                        pe.wait_ge(s["t6_lo"], t)
                    for k in range(3):
                        mm = pe.transpose(ps_t6[:, C * k:C * k + C], u_sb[:, (t + 1) % 2, C * k:C * k + C],
                                          ident[:, :])
                    mm.then_inc(s["t6_mm"], 1)

        @block.vector
        def _(dve):
            link = chained(dve, "dve")

            def t1_low(n):
                dve.wait_ge(s["t1_hi"], n + 1)
                q = t1_hi[:, :, 2:2 + J, n].bitcast(F32).rearrange("p g j -> p j g")
                dve.tensor_tensor(t1_lo[:, :, 2:2 + J, n].rearrange("p g j -> p j g"),
                                  ps_t1[n % 2][:, :].rearrange("p (j g) -> p j g", g=G), q,
                                  ALU.subtract).then_inc(s["t1_lo"], 1)

            dve.wait_ge(s["p3_hi"], 1)
            dve.tensor_tensor(p3_lo[0:CI * KD, :], p3_rows[0:CI * KD, :], p3_hi[0:CI * KD, :].bitcast(F32),
                              ALU.subtract).then_inc(s["p3_lo"], 1)
            dve.wait_ge(s["p4_hi"], 1)
            dve.tensor_tensor(p4_lo[0:CI * K4, :], ps_sel[1][0:CI * K4, 0:C], p4_hi[0:CI * K4, :].bitcast(F32),
                              ALU.subtract).then_inc(s["p4_lo"], 1)
            for n in range(N):
                k = n // 2
                src = x_ring[:, k % XR, n % 2, :]
                if n % 2 == 0:
                    dve.wait_ge(x_in[k], 16 * CI)
                if n >= 2:
                    dve.wait_ge(s["t1_mm"], n - 1)
                dve.transpose(xa[:, n % 2], src.rearrange("p (h w) -> p w h", w=W)).then_inc(s["xa"], 1)
                for hh in range(2):
                    ins = dve.bn_stats(st1[:, n, 6 * hh:6 * hh + 6], src[:, HALF * hh:HALF * hh + HALF])
                ins.then_inc(s["x_used"], 1)
                if n >= 1:
                    t1_low(n - 1)
            t1_low(N - 1)
            t1_low(N)
            dve.wait_ge(s["w_tr"], 1)
            link(dve.tensor_copy(w_f[:, 0, :], ps_sel[0][:, 0:C]))
            link(dve.tensor_scalar(w_det[:, :, :], ps_sel[0][:, C:4 * C].rearrange("p (k c) -> p k c", k=3),
                                   1.0 / 32, None, ALU.mult))
            w1, w2, w3 = (w_det[:, k, :] for k in range(3))
            link(dve.tensor_tensor(w_f[:, 1, :], w2, w3, ALU.add))
            link(dve.tensor_tensor(w_f[:, 3, :], w2, w3, ALU.subtract))
            link(dve.tensor_tensor(w_f[:, 2, :], w1, w_f[:, 1, :], ALU.subtract))
            link(dve.tensor_tensor(w_f[:, 1, :], w1, w_f[:, 1, :], ALU.add))
            link(dve.scalar_tensor_tensor(w_f[:, 4, :], w1, -1.0, w_f[:, 3, :], ALU.mult, ALU.subtract))
            dve.scalar_tensor_tensor(w_f[:, 3, :], w_f[:, 3, :], 2.0, w_f[:, 4, :],
                                     ALU.mult, ALU.add).then_inc(s["w_f"], 1)
            dve.wait_ge(s["w_hi"], 1)
            dve.tensor_tensor(w_lo[:, :, :], w_f[:, :, :], w_hi[:, :, :].bitcast(F32),
                              ALU.subtract).then_inc(s["w_lo"], 1)

            def split_low(g):
                dve.wait_ge(s["s_hi"], g + 1)
                if g >= 2:
                    dve.wait_ge(s["conv"], g - 1)
                if g >= 4:
                    dve.wait_ge(s["t4_mm"], g - 3)
                dve.tensor_tensor(s3_lo[:, g % 2, :], s3_f[:, g % 2].rearrange("p s c m -> p (s c m)"),
                                  s3_hi[:, g % 2, :].bitcast(F32), ALU.subtract)
                dve.tensor_tensor(s4_lo[:, g % 4, :], s4_f[:, g % 4].rearrange("p v m -> p (v m)"),
                                  s4_hi[:, g % 4, :].bitcast(F32), ALU.subtract).then_inc(s["s_lo"], 1)

            split_low(0)
            for g in range(G):
                if g + 1 < G:
                    split_low(g + 1)
                dve.wait_ge(s["t3_hi"], g + 1)
                dve.tensor_tensor(t3_lo[:, g % 2, :], ps_t3[g % 2], t3_hi[:, g % 2, :].bitcast(F32),
                                  ALU.subtract).then_inc(s["t3_lo"], 1)
                if g < N:
                    link(dve.bn_aggr(mv1[:, g, :], st1[:, g, :]))
                if g == N:
                    link(dve.tensor_tensor(rs1[:, 0, :], mv1[:, :, 0], mv1[:, :, 0], ALU.mult))
                    dve.tensor_tensor(mv1[:, :, 1], mv1[:, :, 1], rs1[:, 0, :], ALU.add).then_inc(s["st1"], 1)
            dve.wait_ge(s["gst_mm"], 1)
            link(dve.tensor_copy(gs1[:, :, :].rearrange("p n a -> p (n a)"), ps_st[:, 0:2 * N]))
            link(dve.tensor_tensor(rs1[:, 0, :], gs1[:, :, 0], gs1[:, :, 0], ALU.mult))
            link(dve.tensor_tensor(rs1[:, 0, :], gs1[:, :, 1], rs1[:, 0, :], ALU.subtract))
            dve.tensor_scalar(rs1[:, 0, :], rs1[:, 0, :], 0.0, None, ALU.max).then_inc(s["gst"], 1)
            dve.wait_ge(s["gst_q"], 1)
            link(dve.reciprocal(rs1[:, 1, :], rs1[:, 1, :]))
            link(dve.scalar_tensor_tensor(rs1[:, 2, :], gs1[:, :, 0], -1.0, rs1[:, 1, :], ALU.mult, ALU.mult))
            dve.wait_ge(s["w_in"], 16 * 24)
            link(dve.tensor_scalar(p6_sb[:, :], p6_sb[:, :], float(NF) ** -0.5, None, ALU.mult))
            for d in range(3):
                last = dve.tensor_scalar(a6[:, d, :], rs1[:, 1, :], p6_sb[:, d:d + 1], None, ALU.mult)
            last.then_inc(s["rs1"], 1)

            def rest_of_u(k):
                dst = q6[:, :] if k == 0 else u_sb[:, k % 2, :]
                lo, hi = (p6_sb[:, d:d + 1] if k == 0 else a6[:, d, k - 1:k] for d in (0, 2))
                dve.wait_ge(s["u_act"], k + 1)
                parts = [(C, 2 * C, 0), (G, 3 * G, 2 * C), (1, G - 1, 3 * C - G)]
                for to, n, frm in parts:
                    ins = dve.scalar_tensor_tensor(dst[:, to:to + n], ps_t5[:, frm:frm + n], lo, dst[:, to:to + n],
                                                   ALU.mult, ALU.add)
                link(ins)
                parts = [(0, 2 * C, C), (2 * C, 3 * G, G), (3 * C - G, G - 1, 1)]
                for to, n, frm in parts:
                    ins = dve.scalar_tensor_tensor(dst[:, to:to + n], ps_t5[:, frm:frm + n], hi, dst[:, to:to + n],
                                                   ALU.mult, ALU.add)
                if k == 0:
                    ins.then_inc(s["u"], 1)
                    dve.wait_ge(s["u"], 1)
                else:
                    link(ins)
                    dve.scalar_tensor_tensor(dst, q6[:, :], rs1[:, 2, k - 1:k], dst, ALU.mult, ALU.add
                                             ).then_inc(s["u"], 1)

            rest_of_u(0)
            for t in range(N + 2):
                if t < N:
                    rest_of_u(t + 1)
                n = t - 1
                if 0 <= n < N:
                    b = n % 2
                    for hh in range(2):
                        sl = slice(HALF * hh, HALF * hh + HALF)
                        dve.wait_ge(s["o_mm"] if hh else s["o_half"], n + 1)
                        if hh == 0:
                            dve.wait_ge(s["g1_f"], n + 1)
                        dve.tensor_tensor(x_sb[:, n, sl], x_sb[:, n, sl], ps_o[:, sl], ALU.add).then_inc(s["x1"], 1)
                        dve.wait_ge(s["x1"], 2 * n + hh + 1)
                        ins = dve.bn_stats(st2[:, b, 6 * hh:6 * hh + 6], x_sb[:, n, sl])
                    link(ins)
                    link(dve.bn_aggr(mv2[:, b, :], st2[:, b, :]))
                    dve.scalar_tensor_tensor(mv2[:, b, 1:2], mv2[:, b, 0:1], mv2[:, b, 0:1], mv2[:, b, 1:2],
                                             ALU.mult, ALU.add).then_inc(s["st2"], 1)
                    dve.wait_ge(s["st2_mm"], n + 1)
                    link(dve.tensor_copy(gs2[:, b, :], ps_st[:, 0:2]))
                    link(dve.tensor_tensor(rs2[:, b, 0:1], gs2[:, b, 0:1], gs2[:, b, 0:1], ALU.mult))
                    link(dve.tensor_tensor(rs2[:, b, 1:2], gs2[:, b, 1:2], rs2[:, b, 0:1], ALU.subtract))
                    dve.tensor_scalar(rs2[:, b, 1:2], rs2[:, b, 1:2], 0.0, None, ALU.max).then_inc(s["st2_v"], 1)
                    dve.wait_ge(s["st2_q"], n + 1)
                    link(dve.reciprocal(rs2[:, b, 3:4], rs2[:, b, 2:3]))
                    dve.scalar_tensor_tensor(rs2[:, b, 4:5], gs2[:, b, 0:1], -1.0, rs2[:, b, 3:4],
                                             ALU.mult, ALU.mult).then_inc(s["st2_r"], 1)
                if t < N:
                    dve.wait_ge(s["t6_hi"], t + 1)
                    dve.tensor_tensor(t6_lo[:, :, :], ps_t6[:, 0:NF].rearrange("p (k c) -> p k c", k=3),
                                      t6_hi[:, :, :].bitcast(F32), ALU.subtract).then_inc(s["t6_lo"], 1)
                n = t - 2
                if n >= 0:
                    b = n % 2
                    dve.wait_ge(s["zh"], n + 1)
                    dve.wait_ge(s["y_mm"], n + 1)
                    yr = y_sb[:, n, :].rearrange("p (i a w) -> p a i w", a=2, w=W)
                    pr = ps_y[:, :].rearrange("p (i a w) -> p a i w", a=2, w=W)
                    for a in range(2):
                        ins = dve.tensor_tensor(yr[:, a], pr[:, a], zh[:, b, 2 * a:2 * a + J, :], ALU.add)
                    ins.then_inc(s["y_rd"], 1)
                    dve.wait_ge(s["y_rd"], n + 1)
                    for a in range(2):
                        ins = dve.scalar_tensor_tensor(yr[:, a], zh[:, b, 1:J + 1, :], 3.0, yr[:, a], ALU.mult, ALU.add)
                    ins.then_inc(s["y"], 1)
                    dve.wait_ge(s["y"], n + 1)
                    for hh in range(2):
                        dve.bn_stats(sty[:, n, 6 * hh:6 * hh + 6],
                                     y_sb[:, n, HALF * hh:HALF * hh + HALF]).then_inc(s["sty"], 1)
            dve.wait_ge(s["sty"], 2 * N)
            link(dve.bn_aggr(fin[:, 1:3], sty[:, :, :].rearrange("p n a -> p (n a)")))
            dve.tensor_scalar(fin[:, 2:3], fin[:, 2:3], 0.0, None, ALU.max).then_inc(s["fin_s"], 1)
            dve.wait_ge(s["fin_q"], 1)
            link(dve.reciprocal(fin[:, 4:5], fin[:, 3:4]))
            link(dve.tensor_tensor(fin[:, 5:6], fin[:, 4:5], gb[:, 0:1], ALU.mult))
            link(dve.tensor_tensor(fin[:, 7:8], fin[:, 1:2], fin[:, 5:6], ALU.mult))
            dve.tensor_tensor(fin[:, 6:7], gb[:, 1:2], fin[:, 7:8], ALU.subtract).then_inc(s["fin"], 1)
            for n in range(N):
                dve.wait_ge(s["relu"], n + 1)
                dve.tensor_tensor(x_sb[:, n, :], x_sb[:, n, :], y_sb[:, n, :], ALU.add).then_inc(s["res"], 1)


INPUTS = {"x": "x", "p1": "L0_conv_p1", "p3": "L0_conv_p3", "p4": "L0_conv_p4", "p5": "L0_conv_p5",
          "p6": "L0_conv_p6", "conv_w": "L1_conv_conv_w", "gamma": "L1_conv_gamma", "beta": "L1_conv_beta"}


def kernel(x, L0_conv_p1, L0_conv_p3, L0_conv_p4, L0_conv_p5, L0_conv_p6, L1_conv_conv_w, L1_conv_gamma,
           L1_conv_beta):
    import numpy as np
    import concourse.bacc as bacc
    from concourse.bass_utils import run_bass_kernel_spmd

    given = [x, L0_conv_p1, L0_conv_p3, L0_conv_p4, L0_conv_p5, L0_conv_p6, L1_conv_conv_w, L1_conv_gamma,
             L1_conv_beta]
    nc = bacc.Bacc("TRN2", target_bir_lowering=False, num_devices=1)
    arrays = {"in_" + k: np.ascontiguousarray(v) for k, v in zip(INPUTS, given)}
    args = [nc.dram_tensor(k, v.shape, mybir.dt.from_np(v.dtype), kind="ExternalInput").ap()
            for k, v in arrays.items()]
    out = nc.dram_tensor("out", (N, C, H, W), F32, kind="ExternalOutput").ap()
    build(nc, *args, out)
    result = run_bass_kernel_spmd(nc, [arrays], core_ids=[0])
    return result.results[0]["out"]
```

```python
import concourse.bass as bass
from concourse import mybir
from contextlib import ExitStack

F32 = mybir.dt.float32
F32R = mybir.dt.float32r
ALU = mybir.AluOpType
ACT = mybir.ActivationFunctionType

N, C, H, W = 16, 128, 32, 32
HW = H * W
CI = 4
G = C // CI
E = 16
KD, KX = 9, 9
K4 = 5
NF = 3 * C
J = W // 2
JP = J + 4
NO = N + 1
TAPS = 5
SHIFTS = 2 * TAPS
NB, GB = 4, 8
JC, JL = 4, 4
GN_EPS = 1e-5
BN_EPS = 1e-5
HALF = HW // 2
ZP = J + 2
BY_POOL = 6
WARM, WARM_LAST = 13, 3
PIECES = [(0, slice(0, HALF)), (0, slice(HALF, HW))] + [(n, slice(0, HW)) for n in range(1, N)]
STORES = [(0, 1), (1, 2)] + [(n, n + 2) for n in range(2, N, 2)]
LO_BY_POOL = [2, 3, 4, 5, 6, 7, 8, 9, 11, 13]
COLUMNS = (2, 2, 2, 2, 2, 2, 2, 2)
P5_AT = 7
AFTER = len(COLUMNS)
LATE = 6
GST_AT = 2 * LATE + N // 2 + 1
XR = 3


def build(nc, x, p1, p3, p4, p5, p6, conv_w, gamma, beta, out):
    ctx = ExitStack()
    with ctx:
        def sem(name):
            return ctx.enter_context(nc.semaphore(name))

        base = -(-nc.sbuf_base // 32) * 32
        whole = ctx.enter_context(nc.sbuf_tensor("whole", [128, (nc.sbuf_top - base) // 4 - 8], F32))
        cursor = [base]

        def put(name, shape, dtype=F32):
            t = nc.alloc_sbuf_tensor_at(name, [128] + list(shape), dtype, offset=cursor[0])
            n = 4
            for k in shape:
                n *= k
            cursor[0] += -(-n // 32) * 32
            return t

        ident = put("ident", [128])
        g_mean = put("g_mean", [CI, G])
        ci_mask = put("ci_mask", [CI])
        v_mask = put("v_mask", [2])
        p6_sb = put("p6_sb", [3])
        a6 = put("a6", [3, N])
        gb = put("gb", [2])
        sty = put("sty", [N, 12])
        st1 = sty
        mv1 = put("mv1", [N, 2])
        gs1 = put("gs1", [N, 2])
        rs1 = put("rs1", [3, N])
        st2 = put("st2", [2, 12])
        mv2 = put("mv2", [2, 2])
        gs2 = put("gs2", [2, 2])
        rs2 = put("rs2", [2, 5])
        fin = put("fin", [8])
        minus_half = put("minus_half", [1])
        p5_sb = put("p5_sb", [JC, NF])
        w_hi = put("w_hi", [5, C], F32R)
        w_lo = put("w_lo", [5, C], F32R)

        region_d = cursor[0]
        x_ring = put("x_ring", [XR, 2, HW])
        xa = put("xa", [2, W, G])
        p4_raw = put("p4_raw", [CI, 32])
        p4_rows = put("p4_rows", [C])
        p1_blk = put("p1_blk", [CI * E])
        mask8 = put("mask8", [8])
        in_d = cursor[0]
        cursor[0] = region_d
        d_sb = put("d_sb", [JC, C, NO])
        region_s = cursor[0]
        assert in_d <= region_s

        t1_hi = put("t1_hi", [G, JP, NO], F32R)
        t1_lo = put("t1_lo", [G, JP, NO], F32R)
        toe3 = put("toe3", [G, SHIFTS, E])
        at_toe4 = cursor[0]
        toe4 = put("toe4", [G, CI, E])
        at_s3 = cursor[0]
        s3_f = put("s3_f", [2, SHIFTS, CI, E])
        s3_hi = put("s3_hi", [2, SHIFTS * CI * E], F32R)
        s3_lo = put("s3_lo", [2, SHIFTS * CI * E], F32R)
        s4_f = put("s4_f", [4, CI, 2, E])
        s4_hi = put("s4_hi", [4, 128], F32R)
        s4_lo = put("s4_lo", [4, 128], F32R)
        at_t3 = cursor[0]
        t3_hi = put("t3_hi", [2, J * NO], F32R)
        t3_lo = put("t3_lo", [2, J * NO], F32R)
        at_t4 = cursor[0]
        t4_out = put("t4_out", [2, JL, JC, GB, NO])
        p3_rows = put("p3_rows", [G * 11])
        p3_hi = put("p3_hi", [G * 11], F32R)
        p3_lo = put("p3_lo", [G * 11], F32R)
        assert cursor[0] <= nc.sbuf_top
        cursor[0] = at_toe4
        sel_f = put("sel_f", [E, CI, E])
        assert cursor[0] <= at_s3
        cursor[0] = at_s3
        w_perm = put("w_perm", [4, C])
        one_s3 = 4 * SHIFTS * CI * E
        cursor[0] = at_s3 + one_s3
        t1_f = [put("t1_f0", [G, J])]
        p5_raw = put("p5_raw", [JC, NF])
        w_raw = put("w_raw", [4 * C])
        assert cursor[0] == at_s3 + 5 * one_s3
        t1_f.append(put("t1_f1", [G, J]))
        w_det = put("w_det", [4, C])
        w_f = put("w_f", [5, C])
        assert cursor[0] <= at_t3
        cursor[0] = at_t3
        ones_row = put("ones_row", [HALF])
        cursor[0] = at_t4
        sel3 = put("sel3", [E, 3, CI * E], F32R)
        sel4 = put("sel4", [E, CI, E])

        cursor[0] = region_s
        x_sb = put("x_sb", [N, HW])
        y_sb = put("y_sb", [N, HW])
        g1_hi = put("g1_hi", [(H + 2) * W], F32R)
        g1_lo = put("g1_lo", [(H + 2) * W], F32R)
        g2_hi = put("g2_hi", [HW], F32R)
        g2_lo = put("g2_lo", [HW], F32R)
        t6_hi = put("t6_hi", [3, C], F32R)
        t6_lo = put("t6_lo", [3, C], F32R)
        u_sb = put("u_sb", [2, NF])
        q6 = put("q6", [NF])
        zp = put("zp", [J, ZP])
        z3 = put("z3", [2, J, J])
        zh = put("zh", [2, ZP, W])
        assert cursor[0] <= nc.sbuf_top
        cursor[0] = region_s + 4 * N * HW
        d_split = put("d_split", [NO, 2, JC, C], F32R)
        cursor[0] = region_s + 4 * (N - 4) * HW
        p5_first = [put("p5_first_hi", [JC, NF], F32R), put("p5_first_lo", [JC, NF], F32R)]
        assert cursor[0] <= region_s + 4 * N * HW
        cursor[0] = region_d
        p5_rest = [put("p5_rest_hi", [JC, NF], F32R), put("p5_rest_lo", [JC, NF], F32R)]
        assert cursor[0] <= region_s

        bank = [ctx.enter_context(nc.psum_tensor(f"bank{i}", [128, 512], F32)) for i in range(4)]
        wide = [ctx.enter_context(nc.psum_tensor(f"wide{i}", [128, 1024], F32)) for i in range(2)]
        ps_t1 = [bank[0], bank[1]]
        ps_sel = [bank[2], bank[3]]
        ps_t3 = [wide[0][:, 0:J * NO], wide[0][:, 512:512 + J * NO]]
        ps_t4 = [wide[1][:, 0:J * NO], wide[1][:, 512:512 + J * NO]]
        ps_t5, ps_t6, ps_z, ps_st = bank
        ps_o, ps_y = wide

        names = ("const zeros sel_f sel4 sel3_pad sel3 sel_rows w_in p5_in p6_in p1_in xa x_used "
                 "t1_mm t1_hi t1_lo t1_f t1_lo_pool p3_hi p3_lo p4_tr p4_ev "
                 "d_in_pool d_hi d_lo d_lo_pool p5_first_hi p5_first_lo p5_rest_hi p5_rest_lo u_part "
                 "sel_mm sel_ev w_pm p5_pm w_f w_hi w_lo s_f s_hi s_lo conv t3_hi t3_lo t4_mm t4_ev "
                 "st1 gst_mm gst gst_q rs1 t5 u_act u t6_mm t6_hi t6_lo g1_f g1_hi g1_lo o_half o_mm x1 "
                 "st2 st2_mm st2_v st2_r g2_hi g2_lo z_mm z_ev zh y_mm y_rd y sty "
                 "fin_s fin_q fin relu res dve pool stored").split()
        s = {n: sem("s_" + n) for n in names}
        x_in = [sem(f"s_x_in{k}") for k in range(N // 2)]
        d_in = [sem(f"s_d_in{b}") for b in range(NB)]

        def chained(eng, name):
            count = [0]

            def link(ins):
                count[0] += 1
                ins.then_inc(s[name], 1)
                eng.wait_ge(s[name], count[0])
            return link

        def split_product(ps, w, m, start, stop):
            nc.tensor.matmul(ps, w[0], m[0], start=start, stop=False)
            nc.tensor.matmul(ps, w[0], m[1], start=False, stop=False)
            return nc.tensor.matmul(ps, w[1], m[0], start=False, stop=stop)

        def t5_bank(k):
            return (ps_t5, ps_z, ps_st)[k] if k < 3 else ps_t5

        def lo_count(i):
            return sum(k not in LO_BY_POOL for k in range(i + 1))

        def wait_d(eng):
            for b in range(NB):
                eng.wait_ge(d_in[b], 16 * (JL * CI - (BY_POOL if b == NB - 1 else 0)))
            eng.wait_ge(s["d_in_pool"], 16 * BY_POOL)

        SPLITS = [(0, 0, NO, False), (1, 0, NO, False), (2, N, NO, False), (2, 0, 2, False), (2, 2, N, True),
                  (3, N, NO, False), (3, 0, 2, False), (3, 2, N, True)]

        def split_views(b, n0, n1):
            def pick(v):
                return v.rearrange("p n j (co g) -> p n (j co) g", co=CI)[:, :, :, GB * b:GB * b + GB]
            return (pick(d_sb[:, :, :, n0:n1].rearrange("p j c n -> p n j c")),
                    pick(d_split[:, n0:n1, 0]), pick(d_split[:, n0:n1, 1]))

        block = ctx.enter_context(nc.Block())

        def load_x(eng, dst, k):
            for ci in range(CI):
                eng.dma_start(dst[G * ci:G * ci + G],
                              x[2 * k:2 * k + 2].rearrange("n (g c) h w -> c g n (h w)", c=CI)[ci]
                              ).then_inc(x_in[k], 16)

        blocks = [(jl, co) for jl in range(JL) for co in range(CI)]

        def shuffle(eng, b, jl, co, done):
            eng.dma_start(
                d_sb[32 * jl:32 * jl + 32, :, G * co + GB * b:G * co + GB * b + GB, :].rearrange(
                    "p j g n -> p j (g n)"),
                t4_out[32 * co:32 * co + 32, b % 2, jl].rearrange("p j g n -> p j (g n)")).then_inc(done, 16)

        @block.sync
        def _(sp):
            load_x(sp, x_ring[:, 0], 0)
            sp.wait_ge(s["zeros"], 1)
            for ci in range(CI):
                sp.dma_start(p1_blk[32 * ci:32 * ci + 32, E * ci:E * ci + E], p1).then_inc(s["p1_in"], 16)
            load_x(sp, x_ring[:, 1], 1)
            for ci in range(CI):
                sp.dma_start(p3_rows[32 * ci:32 * ci + KD, :].rearrange("p (g s) -> p g s", g=G)[:, :, 1:1 + KX],
                             p3.rearrange("(g c) o y x -> c y g (o x)", c=CI)[ci]).then_inc(s["sel_rows"], 16)
            sp.dma_start(p4_raw[:, :, 0:K4], p4.rearrange("c i y x -> c i (y x)")).then_inc(s["sel_rows"], 16)
            for k in range(2, N // 2):
                if k >= XR:
                    sp.wait_ge(s["x_used"], 4 * (k - XR + 1))
                load_x(sp, x_ring[:, k % XR], k)
                for ci in range(CI):
                    q = slice(G * ci, G * ci + G)
                    if k == 2:
                        sp.dma_start(w_raw[q, :], conv_w.rearrange("(g c) f -> c g f", c=CI)[ci]
                                     ).then_inc(s["w_in"], 16)
                    elif k == 3:
                        for v in range(2):
                            sp.dma_start(p5_raw[32 * ci + 16 * v:32 * ci + 16 * v + 16, :, :],
                                         p5.rearrange("e (j r) o f -> r e j (o f)", r=2 * JL)[2 * ci + 1 - v]
                                         ).then_inc(s["p5_in"], 16)
                    elif k == 5:
                        sp.dma_start(p6_sb[q, :], p6.rearrange("(g c) a b d -> c g (a b d)", c=CI)[ci]
                                     ).then_inc(s["p6_in"], 16)
                        sp.dma_start(gb[q, 0:1], gamma.rearrange("(g c a) -> c g a", c=CI, a=1)[ci],
                                     allow_slow_non_contiguous=True).then_inc(s["p6_in"], 16)
                        sp.dma_start(gb[q, 1:2], beta.rearrange("(g c a) -> c g a", c=CI, a=1)[ci],
                                     allow_slow_non_contiguous=True).then_inc(s["p6_in"], 16)
            for b in range(NB):
                if b == NB - 1:
                    sp.wait_ge(s["conv"], G)
                    load_x(sp, x_sb[:, 0:2, :], 0)
                sp.wait_ge(s["t4_ev"], GB * (b + 1))
                if b == 0:
                    sp.wait_ge(s["t1_mm"], NO)
                    sp.wait_ge(s["x_used"], 2 * N)
                for jl, co in blocks if b < NB - 1 else blocks[BY_POOL:]:
                    shuffle(sp, b, jl, co, d_in[b])
            for k in range(1, N // 2):
                if k == N // 2 - 2:
                    sp.wait_ge(s["t5"], 3)
                load_x(sp, x_sb[:, 2 * k:2 * k + 2, :], k)
            for n, end in STORES:
                sp.wait_ge(s["res"], end + 1)
                for ci in range(CI):
                    sp.dma_start(out[n:end].rearrange("n (g c) h w -> c g n (h w)", c=CI)[ci],
                                 x_sb[G * ci:G * ci + G, n:end, :]).then_inc(s["stored"], 16)
            sp.wait_ge(s["stored"], 16 * CI * len(STORES))

        @block.gpsimd
        def _(pool):
            link = chained(pool, "pool")
            pool.memset(p1_blk[:, :], 0.0)
            pool.memset(p4_raw[:, :, :], 0.0)
            pool.memset(p3_rows[:, :], 0.0).then_inc(s["zeros"], 1)
            pool.memset(ident[:, :], 0.0)
            pool.memset(sel_f[:, :, :, :], 0.0)
            pool.memset(sel4[:, :, :, :], 0.0)
            pool.memset(mask8[:, :], 1.0)
            pool.memset(v_mask[:, :], 1.0)
            pool.memset(minus_half[:, :], -0.5)
            link(pool.memset(ones_row[:, :], 1.0))
            pool.affine_select(out=ident[:, :], in_=ident[:, :], compare_op=ALU.not_equal, fill=1.0,
                               base=0, pattern=[[-1, 128]], channel_multiplier=1).then_inc(s["const"], 1)
            for tile, k, name in ((sel_f, KD, "sel_f"), (sel4, K4, "sel4")):
                assert E - 1 + k // 2 < 32 - (E - 1 - k // 2)
                pool.affine_select(out=tile[:, :, :, :], in_=tile[:, :, :, :], compare_op=ALU.not_equal, fill=1.0,
                                   base=-(k // 2), pattern=[[1, E], [-32, CI], [-1, E]],
                                   channel_multiplier=1).then_inc(s[name], 1)
                if tile is sel_f:
                    pool.memset(sel3[:, :, 0:3:2, :].bitcast(F32), 0.0).then_inc(s["sel3_pad"], 1)
            for t in (t1_hi, t1_lo):
                pool.memset(t[:, :, 0:2, :].bitcast(F32), 0.0)
                pool.memset(t[:, :, JP - 2:JP, :].bitcast(F32), 0.0).then_inc(s["zeros"], 1)
            link(pool.memset(g_mean[:, :, :], 0.0))
            for m in range(CI):
                link(pool.affine_select(out=g_mean[:, :, :], in_=g_mean[:, :, :], compare_op=ALU.not_equal,
                                        fill=1.0 / CI, base=-G * m, pattern=[[0, CI], [-1, G]],
                                        channel_multiplier=1))
            link(pool.affine_select(out=mask8[:, :], in_=mask8[:, :], compare_op=ALU.is_ge, fill=0.0, base=0,
                                    pattern=[[-16, 8]], channel_multiplier=1))
            link(pool.affine_select(out=mask8[:, :], in_=mask8[:, :], compare_op=ALU.is_ge, fill=0.0, base=15,
                                    pattern=[[16, 8]], channel_multiplier=-1))
            link(pool.tensor_tensor(ci_mask[:, :], mask8[:, 0:4], mask8[:, 4:8], ALU.add))
            link(pool.affine_select(out=v_mask[:, :], in_=v_mask[:, :], compare_op=ALU.is_ge, fill=0.0, base=63,
                                    pattern=[[128, 2]], channel_multiplier=-1))
            link(pool.affine_select(out=v_mask[:, :], in_=v_mask[:, :], compare_op=ALU.is_ge, fill=0.0, base=64,
                                    pattern=[[-128, 2]], channel_multiplier=1))
            def t1_low(i):
                pool.wait_ge(s["t1_f"], LO_BY_POOL.index(i) + 1)
                pool.tensor_tensor(t1_lo[:, :, 2:2 + J, (i - 1) % NO], t1_f[LO_BY_POOL.index(i) % 2][:, :, :],
                                   t1_hi[:, :, 2:2 + J, (i - 1) % NO].bitcast(F32),
                                   ALU.subtract).then_inc(s["t1_lo_pool"], 1)

            for i in LO_BY_POOL[:LO_BY_POOL.index(8) + 1]:
                t1_low(i)
            pool.wait_ge(s["sel_ev"], E + 1)
            w1, w2, w3, minus_w1 = (w_det[:, k, :] for k in range(4))
            link(pool.tensor_tensor(w_f[:, 1, :], w2, w3, ALU.add))
            link(pool.tensor_tensor(w_f[:, 3, :], w2, w3, ALU.subtract))
            pool.tensor_tensor(w_f[:, 2, :], w1, w_f[:, 1, :], ALU.subtract)
            link(pool.tensor_tensor(w_f[:, 4, :], minus_w1, w_f[:, 3, :], ALU.subtract))
            pool.tensor_tensor(w_f[:, 1, :], w1, w_f[:, 1, :], ALU.add)
            pool.tensor_tensor(w_f[:, 3, :], minus_w1, w_f[:, 3, :], ALU.add).then_inc(s["w_f"], 1)
            for i in (9, 10, 11):
                if i in LO_BY_POOL:
                    t1_low(i)
            pool.wait_ge(s["w_hi"], 1)
            pool.tensor_tensor(w_lo[:, :, :], w_f[:, :, :], w_hi[:, :, :].bitcast(F32),
                               ALU.subtract).then_inc(s["w_lo"], 1)
            for i in range(12, 14):
                if i in LO_BY_POOL:
                    t1_low(i)
            pool.wait_ge(s["p5_pm"], JC)
            pool.wait_ge(s["w_lo"], 1)
            pool.wait_ge(s["sel_ev"], E + 5)
            for g in range(G):
                if g == 1:
                    for i in range(14, NO):
                        if i in LO_BY_POOL:
                            t1_low(i)
                    pool.wait_ge(s["t1_lo_pool"], len(LO_BY_POOL))
                if g >= 2:
                    pool.wait_ge(s["s_lo"], g - 1)
                pool.tensor_tensor(
                    s3_f[:, g % 2], toe3[:, g].unsqueeze(2).broadcast_to([128, SHIFTS, CI, E]),
                    ci_mask[:, :].unsqueeze(1).unsqueeze(3).broadcast_to([128, SHIFTS, CI, E]), ALU.mult)
                pool.tensor_tensor(
                    s4_f[:, g % 4], toe4[:, g].unsqueeze(2).broadcast_to([128, CI, 2, E]),
                    v_mask[:, :].unsqueeze(1).unsqueeze(3).broadcast_to([128, CI, 2, E]), ALU.mult
                    ).then_inc(s["s_f"], 1)
            pool.wait_ge(s["gst"], 1)
            pool.tensor_tensor(rs1[:, 1, :], rs1[:, 0, :], minus_half[:, :].broadcast_to([128, N]),
                               ALU.pow).then_inc(s["gst_q"], 1)
            pool.wait_ge(s["t4_ev"], G)
            for jl, co in blocks[:BY_POOL]:
                shuffle(pool, NB - 1, jl, co, s["d_in_pool"])
            def t4_low(i):
                b, n0, n1, _ = SPLITS[i]
                pool.wait_ge(s["d_hi"], i + 1)
                src, hi, lo = split_views(b, n0, n1)
                pool.tensor_tensor(lo, src, hi.bitcast(F32), ALU.subtract).then_inc(s["d_lo_pool"], 1)

            t4_low(4)
            pool.wait_ge(s["t5"], 1)
            for t in (g1_hi, g1_lo):
                v = t[:, :].bitcast(F32).rearrange("p (i w) -> p i w", w=W)
                pool.memset(v[:, 0:H + 2:H + 1, :], 0.0).then_inc(s["zeros"], 1)
            t4_low(7)

            def g1_low(n):
                pool.wait_ge(s["g1_hi"], n + 1)
                pool.tensor_tensor(g1_lo[:, W:W + HW], y_sb[:, n, :], g1_hi[:, W:W + HW].bitcast(F32),
                                   ALU.subtract).then_inc(s["g1_lo"], 1)

            def norm_factors(n):
                b = n % 2
                mean, m2, var, rstd, bias = gs2[:, b, 0:1], *(rs2[:, b, i:i + 1] for i in (0, 1, 3, 4))
                pool.wait_ge(s["st2_v"], n + 1)
                link(pool.tensor_tensor(m2, mean, mean, ALU.mult))
                link(pool.tensor_tensor(var, gs2[:, b, 1:2], m2, ALU.subtract))
                link(pool.tensor_scalar(var, var, 0.0, GN_EPS, ALU.max, ALU.add))
                link(pool.tensor_tensor(rstd, var, minus_half[:, :], ALU.pow))
                pool.tensor_scalar(bias, mean, -1.0, rstd, ALU.mult, ALU.mult).then_inc(s["st2_r"], 1)

            def z_columns(n):
                pool.wait_ge(s["z_ev"], n + 1)
                if n >= 2:
                    pool.wait_ge(s["y"], n - 1)
                rows = zh[:, n % 2, 1:J + 1, :].rearrange("p i (j a) -> p i j a", a=2)
                pool.tensor_tensor(rows[:, :, :, 0], z3[:, n % 2], zp[:, :, 0:J], ALU.add)
                link(pool.tensor_tensor(rows[:, :, :, 1], z3[:, n % 2], zp[:, :, 2:ZP], ALU.add))
                pool.tensor_copy(zh[:, n % 2, 0:ZP:ZP - 1, :],
                                 zh[:, n % 2, 1:J + 1:J - 1, :]).then_inc(s["zh"], 1)

            def g2_low(n):
                pool.wait_ge(s["g2_hi"], n + 1)
                pool.tensor_tensor(g2_lo[:, :], y_sb[:, n, :], g2_hi[:, :].bitcast(F32),
                                   ALU.subtract).then_inc(s["g2_lo"], 1)

            for t in range(N + 2):
                if 1 <= t < N:
                    g1_low(t)
                if t == 0:
                    pool.wait_ge(s["p5_rest_hi"], 1)
                    pool.tensor_tensor(p5_rest[1][:, :, :], p5_sb[:, :, :], p5_rest[0][:, :, :].bitcast(F32),
                                       ALU.subtract).then_inc(s["p5_rest_lo"], 1)
                if 1 <= t <= N:
                    norm_factors(t - 1)
                if t >= 2:
                    z_columns(t - 2)
                if 1 <= t < N:
                    g2_low(t - 1)
            pool.wait_ge(s["fin_s"], 1)
            pool.tensor_tensor(fin[:, 4:5], fin[:, 2:3], minus_half[:, :], ALU.pow).then_inc(s["fin_q"], 1)

        @block.scalar
        def _(act):
            def t1_high(i):
                act.wait_ge(s["t1_mm"], i + 1)
                act.copy(t1_hi[:, :, 2:2 + J, (i - 1) % NO].rearrange("p g j -> p j g"),
                         ps_t1[i % 2][:, :].rearrange("p (j g) -> p j g", g=G)).then_inc(s["t1_hi"], 1)
                if i in LO_BY_POOL:
                    b = LO_BY_POOL.index(i)
                    if b >= 2:
                        act.wait_ge(s["t1_lo_pool"], b - 1)
                    act.copy(t1_f[b % 2][:, :, :].rearrange("p g j -> p j g"),
                             ps_t1[i % 2][:, :].rearrange("p (j g) -> p j g", g=G)).then_inc(s["t1_f"], 1)

            def toe3_evacuate(m):
                act.wait_ge(s["sel_mm"], m + 1)
                act.copy(toe3[:, :, :, m], ps_sel[m % 2][:, 0:G * SHIFTS].rearrange("p (g s) -> p g s", g=G)
                         ).then_inc(s["sel_ev"], 1)

            def toe4_evacuate(q):
                act.wait_ge(s["sel_mm"], E + q + 2)
                act.copy(toe4[:, :, :, 4 * q:4 * q + 4].rearrange("p g c m -> p m g c"),
                         ps_sel[(q + 1) % 2][:, :].rearrange("p (m g c) -> p m g c", m=4, g=G)).then_inc(s["sel_ev"], 1)

            def split_high(g):
                act.wait_ge(s["s_f"], g + 1)
                if g >= 2:
                    act.wait_ge(s["conv"], g - 1)
                if g >= 4:
                    act.wait_ge(s["t4_mm"], g - 3)
                act.copy(s3_hi[:, g % 2, :], s3_f[:, g % 2].rearrange("p s c m -> p (s c m)"))
                act.copy(s4_hi[:, g % 4, :], s4_f[:, g % 4].rearrange("p c v m -> p (c v m)")).then_inc(s["s_hi"], 1)

            act.wait_ge(s["sel_f"], 1)
            act.copy(sel3[:, :, 1], sel_f[:, :, :, :].rearrange("p m c e -> p m (c e)")).then_inc(s["sel3"], 1)
            t1_high(0)
            for n in range(N):
                t1_high(n + 1)
                if n == 0:
                    act.wait_ge(s["sel_rows"], 16 * (CI + 1))
                    act.copy(p3_hi[:, :], p3_rows[:, :]).then_inc(s["p3_hi"], 1)
                    act.wait_ge(s["p4_tr"], 1)
                    act.copy(p4_rows[:, :], ps_sel[1][:, 0:C]).then_inc(s["p4_ev"], 1)
                if n < len(COLUMNS):
                    for m in range(sum(COLUMNS[:n]), sum(COLUMNS[:n + 1])):
                        toe3_evacuate(m)
                    if n == 6:
                        act.wait_ge(s["w_in"], 16 * CI)
                        act.copy(w_perm[:, :, :].rearrange("p k (c g) -> p k c g", c=CI),
                                 w_raw[:, :].rearrange("p (k g c) -> p k c g", k=4, c=CI)).then_inc(s["w_pm"], 1)
                elif n < AFTER + 4:
                    if n == AFTER:
                        act.wait_ge(s["sel_mm"], E + 1)
                        act.copy(w_f[:, 0, :], ps_sel[0][:, 0:C])
                        act.mul(w_det[:, 0:3, :], ps_sel[0][:, C:4 * C].rearrange("p (k c) -> p k c", k=3), 1.0 / 32)
                        act.mul(w_det[:, 3, :], ps_sel[0][:, C:2 * C], -1.0 / 32).then_inc(s["sel_ev"], 1)
                    toe4_evacuate(n - AFTER)
                    if n == AFTER + 2:
                        act.wait_ge(s["w_f"], 1)
                        act.copy(w_hi[:, :, :], w_f[:, :, :]).then_inc(s["w_hi"], 1)
                if P5_AT <= n < P5_AT + JC:
                    if n == P5_AT:
                        act.wait_ge(s["p5_in"], 16 * 2 * JL)
                    act.copy(p5_sb[:, n - P5_AT, :].rearrange("p (k c g) -> p k c g", k=3, c=CI),
                             p5_raw[:, n - P5_AT, :].rearrange("p (g c k) -> p k c g", c=CI, k=3)
                             ).then_inc(s["p5_pm"], 1)

            def t4_evacuate(g):
                b = g // GB
                act.wait_ge(s["t4_mm"], g + 1)
                if b >= 2 and g % GB == 0:
                    act.wait_ge(d_in[b - 2], 16 * JL * CI)
                act.copy(t4_out[:, b % 2, :, :, g % GB, :].rearrange("p jl jc n -> p jc jl n"),
                         ps_t4[g % 2].rearrange("p (jc jl n) -> p jc jl n", jc=JC, jl=JL)).then_inc(s["t4_ev"], 1)

            split_high(0)
            for g in range(G):
                if g + 1 < G:
                    split_high(g + 1)
                act.wait_ge(s["conv"], g + 1)
                if g >= 2:
                    act.wait_ge(s["t4_mm"], g - 1)
                act.copy(t3_hi[:, g % 2, :], ps_t3[g % 2]).then_inc(s["t3_hi"], 1)
                if g >= 1:
                    t4_evacuate(g - 1)
            act.copy(p5_first[0][:, 0:2, :], p5_sb[:, 0:2, :]).then_inc(s["p5_first_hi"], 1)
            t4_evacuate(G - 1)
            act.copy(p5_first[0][:, 2:4, :], p5_sb[:, 2:4, :]).then_inc(s["p5_first_hi"], 1)
            for b, n0, n1, _ in SPLITS:
                if b < NB - 1:
                    act.wait_ge(d_in[b], 16 * JL * CI)
                elif n0 == N:
                    wait_d(act)
                src, hi, _ = split_views(b, n0, n1)
                act.copy(hi, src).then_inc(s["d_hi"], 1)

            def middle_of_u(k):
                act.wait_ge(s["t5"], k + 1)
                if k >= 3:
                    act.wait_ge(s["t6_mm"], k - 2)
                scale = p6_sb[:, 1:2] if k == 0 else a6[:, 1, k - 1:k]
                dst = q6[:, :] if k == 0 else u_sb[:, k % 2, :]
                act.activation(dst, t5_bank(k)[:, 0:NF], ACT.Identity, scale=scale).then_inc(s["u_act"], 1)

            def g1_full(n):
                act.wait_ge(x_in[n // 2], 2 * 16 * CI)
                act.wait_ge(s["t5"], n + 2)
                act.activation(y_sb[:, n, :], x_sb[:, n, :], ACT.Identity, bias=rs1[:, 2, n:n + 1],
                               scale=rs1[:, 1, n:n + 1]).then_inc(s["g1_f"], 1)

            def g1_high(n):
                act.wait_ge(s["g1_f"], n + 1)
                if n >= 1:
                    act.wait_ge(s["o_mm"], n)
                act.copy(g1_hi[:, W:W + HW], y_sb[:, n, :]).then_inc(s["g1_hi"], 1)

            def t6_high(n):
                act.wait_ge(s["t6_mm"], n + 1)
                if n >= 1:
                    act.wait_ge(s["o_mm"], n)
                act.copy(t6_hi[:, :, :], ps_t6[:, 0:NF].rearrange("p (k c) -> p k c", k=3)).then_inc(s["t6_hi"], 1)

            def averages(n):
                act.wait_ge(s["st2_mm"], n + 1)
                act.copy(gs2[:, n % 2, :], ps_st[:, 0:2]).then_inc(s["st2_v"], 1)

            def z_evacuate(n):
                z = ps_z[:, 0:J * J].rearrange("p (i j) -> p i j", i=J)
                act.wait_ge(s["z_mm"], n + 1)
                if n >= 1:
                    act.wait_ge(s["zh"], n)
                act.copy(zp[:, :, 1:J + 1], z)
                act.copy(zp[:, :, 0:ZP:ZP - 1], z[:, :, 0:J:J - 1])
                act.mul(z3[:, n % 2], z, 3.0).then_inc(s["z_ev"], 1)

            def g2_full_and_high(n):
                act.wait_ge(s["st2_r"], n + 1)
                act.wait_ge(s["g1_lo"], n + 1)
                norm = dict(bias=rs2[:, n % 2, 4:5], scale=rs2[:, n % 2, 3:4])
                if n >= 1:
                    act.wait_ge(s["y_mm"], n)
                act.activation(g2_hi[:, :], x_sb[:, n, :], ACT.Identity, **norm)
                act.activation(y_sb[:, n, :], x_sb[:, n, :], ACT.Identity, **norm).then_inc(s["g2_hi"], 1)

            act.wait_ge(s["rs1"], 1)
            middle_of_u(0)
            middle_of_u(1)
            g1_full(0)
            act.wait_ge(s["zeros"], 5)
            g1_high(0)
            for t in range(N + 2):
                if 1 <= t < N:
                    g1_high(t)
                if t < N:
                    t6_high(t)
                if t + 2 <= N:
                    middle_of_u(t + 2)
                if 1 <= t <= N:
                    averages(t - 1)
                if t >= 2:
                    z_evacuate(t - 2)
                if 1 <= t <= N:
                    g2_full_and_high(t - 1)
                if t == 0:
                    act.wait_ge(s["d_lo"], 6)
                    act.wait_ge(s["d_lo_pool"], 2)
                    act.copy(p5_rest[0][:, :, :], p5_sb[:, :, :]).then_inc(s["p5_rest_hi"], 1)
                if t + 1 < N:
                    g1_full(t + 1)
            act.wait_ge(s["fin"], 1)
            for n, sl in PIECES:
                act.activation(y_sb[:, n, sl], y_sb[:, n, sl], ACT.Relu, bias=fin[:, 6:7],
                               scale=fin[:, 5:6]).then_inc(s["relu"], 1)

        @block.tensor
        def _(pe):
            def t1_product(i):
                if i >= 1:
                    pe.wait_ge(s["xa"], i)
                if i >= 2:
                    if i - 2 in LO_BY_POOL:
                        pe.wait_ge(s["t1_f"], LO_BY_POOL.index(i - 2) + 1)
                    else:
                        pe.wait_ge(s["t1_lo"], lo_count(i - 2))
                for wp in range(2):
                    rhs = xa[:, (i - 1) % 2, wp:W:2, :] if i >= 1 else ones_row[:, :]
                    mm = pe.matmul(ps_t1[i % 2][64 * wp:64 * wp + 64, :], p1_blk[:, :], rhs, start=True, stop=True)
                mm.then_inc(s["t1_mm"], 1)

            def toe3_product(m):
                if m >= 2:
                    pe.wait_ge(s["sel_ev"], m - 1)
                for wp in range(2):
                    w = sel3[:, m, 1 - wp:3 - wp].rearrange("p v q -> p (v q)")
                    for h in (p3_hi, p3_lo):
                        mm = pe.matmul(ps_sel[m % 2][:, 0:G * SHIFTS], w,
                                       h[:, :].rearrange("p (g s) -> p g s", g=G)[:, :, wp:wp + SHIFTS],
                                       start=(wp == 0 and h is p3_hi), stop=(wp == 1 and h is p3_lo))
                mm.then_inc(s["sel_mm"], 1)

            def toe4_product(q):
                pe.wait_ge(s["sel_ev"], E + q)
                for r in range(4):
                    for v in range(2):
                        mm = pe.matmul(ps_sel[(q + 1) % 2][64 * v:64 * v + 64, 128 * r:128 * r + 128],
                                       sel4[:, 4 * q + r].rearrange("p c e -> p (c e)"), p4_rows[:, :],
                                       start=True, stop=True)
                mm.then_inc(s["sel_mm"], 1)

            def w_transposes():
                pe.wait_ge(s["w_pm"], 1)
                pe.wait_ge(s["sel_ev"], E - 1)
                for k in range(4):
                    mm = pe.transpose(ps_sel[0][:, C * k:C * k + C], w_perm[:, k, :], ident[:, :])
                mm.then_inc(s["sel_mm"], 1)

            pe.wait_ge(s["const"], 1)
            pe.wait_ge(s["p1_in"], 64)
            t1_product(0)
            for n in range(N):
                t1_product(n + 1)
                if n == 0:
                    pe.wait_ge(s["sel_rows"], 16 * (CI + 1))
                    pe.transpose(ps_sel[1][:, 0:C], p4_raw[:, :, :].rearrange("p i y -> p (i y)"), ident[:, :]
                                 ).then_inc(s["p4_tr"], 1)
                    pe.wait_ge(s["sel3"], 1)
                    pe.wait_ge(s["sel3_pad"], 1)
                    pe.wait_ge(s["p3_lo"], 1)
                if n < len(COLUMNS):
                    for m in range(sum(COLUMNS[:n]), sum(COLUMNS[:n + 1])):
                        if m == 1:
                            pe.wait_ge(s["p4_ev"], 1)
                        toe3_product(m)
                elif n < AFTER + 4:
                    if n == AFTER:
                        w_transposes()
                        pe.wait_ge(s["sel4"], 1)
                    toe4_product(n - AFTER)

            def t4_product(g):
                pe.wait_ge(s["t3_lo"], g + 1)
                if g >= 2:
                    pe.wait_ge(s["t4_ev"], g - 1)
                split_product(ps_t4[g % 2], (s4_hi[:, g % 4, :], s4_lo[:, g % 4, :]),
                              (t3_hi[:, g % 2, :], t3_lo[:, g % 2, :]), True, True).then_inc(s["t4_mm"], 1)

            pe.wait_ge(s["t1_hi"], NO)
            pe.wait_ge(s["zeros"], 3)
            for g in range(G):
                pe.wait_ge(s["s_hi"], g + 1)
                if g >= 2:
                    pe.wait_ge(s["t3_lo"], g - 1)
                for weights, data, first in ((s3_hi, t1_hi, True), (s3_hi, t1_lo, False), (s3_lo, t1_hi, False)):
                    if weights is s3_lo:
                        pe.wait_ge(s["s_lo"], g + 1)
                    elif data is t1_lo and g == 0:
                        pe.wait_ge(s["t1_lo"], lo_count(N))
                        pe.wait_ge(s["t1_lo_pool"], len(LO_BY_POOL))
                    for t in range(TAPS):
                        mm = pe.matmul(ps_t3[g % 2], weights[:, g % 2, 128 * t:128 * t + 128],
                                       data[:, g, t:t + J, :].rearrange("p j n -> p (j n)"),
                                       start=(first and t == 0), stop=(weights is s3_lo and t == TAPS - 1))
                mm.then_inc(s["conv"], 1)
                if g >= 1:
                    t4_product(g - 1)
                if g == GST_AT + 1:
                    pe.wait_ge(s["st1"], 1)
                    pe.matmul(ps_st[:, 0:2 * N], g_mean[:, :, :].rearrange("p a b -> p (a b)"),
                              mv1[:, :, :].rearrange("p n a -> p (n a)"), start=True, stop=True
                              ).then_inc(s["gst_mm"], 1)
            t4_product(G - 1)
            def t5_product(k):
                if k >= 3:
                    pe.wait_ge(s["u"], k)
                    pe.wait_ge(s["p5_rest_lo"], 1)
                    pe.wait_ge(s["d_lo_pool"], 2)
                else:
                    pe.wait_ge(s["p5_first_lo"], 2)
                pe.wait_ge(s["d_lo"], 5 if k == 0 else 6)
                n, p5_parts = (k - 1) % NO, p5_first if k < 3 else p5_rest
                for jc in range(JC):
                    mm = split_product(t5_bank(k)[:, 0:NF], (d_split[:, n, 0, jc, :], d_split[:, n, 1, jc, :]),
                                       (p5_parts[0][:, jc, :], p5_parts[1][:, jc, :]), jc == 0, jc == JC - 1)
                mm.then_inc(s["t5"], 1)

            def keep_clock(products, bank):
                for i in range(products):
                    pe.matmul(bank[:, 0:NF], g_mean[:, :, :].rearrange("p a b -> p (a b)"), p5_sb[:, 0, :],
                              start=True, stop=True)

            keep_clock(WARM, ps_t6)
            def out_product(n):
                pe.wait_ge(s["t6_lo"], n + 1)
                pe.wait_ge(s["g1_lo"], n + 1)
                for hh in range(2):
                    if n >= 1:
                        pe.wait_ge(s["x1"], 2 * (n - 1) + hh + 1)
                    for k in range(3):
                        lo = (H // 2 * hh + k) * W
                        mm = split_product(ps_o[:, HALF * hh:HALF * hh + HALF], (t6_hi[:, k, :], t6_lo[:, k, :]),
                                           (g1_hi[:, lo:lo + HALF], g1_lo[:, lo:lo + HALF]), k == 0, k == 2)
                    mm.then_inc(s["o_mm"] if hh else s["o_half"], 1)

            def t6_transpose(n):
                pe.wait_ge(s["u"], n + 2)
                if n >= 1:
                    pe.wait_ge(s["t6_lo"], n)
                for k in range(3):
                    mm = pe.transpose(ps_t6[:, C * k:C * k + C], u_sb[:, (n + 1) % 2, C * k:C * k + C], ident[:, :])
                mm.then_inc(s["t6_mm"], 1)

            def group_average(n):
                pe.wait_ge(s["st2"], n + 1)
                if n >= 1:
                    pe.wait_ge(s["st2_v"], n)
                pe.matmul(ps_st[:, 0:2], g_mean[:, :, :].rearrange("p a b -> p (a b)"), mv2[:, n % 2, :],
                          start=True, stop=True).then_inc(s["st2_mm"], 1)

            def z_product(n):
                pe.wait_ge(s["g2_lo"], n + 1)
                if n >= 1:
                    pe.wait_ge(s["z_ev"], n)
                ph = [h[:, :].rearrange("p (i a j b) -> p a b i j", a=2, b=2, i=J) for h in (g2_hi, g2_lo)]
                for q in range(4):
                    mm = split_product(ps_z[:, 0:J * J], (w_hi[:, 1 + q, :], w_lo[:, 1 + q, :]),
                                       [h[:, q // 2, q % 2] for h in ph], q == 0, q == 3)
                mm.then_inc(s["z_mm"], 1)

            def y_product(n):
                if n >= 1:
                    pe.wait_ge(s["y_rd"], n)
                for hh in range(2):
                    q = slice(HALF * hh, HALF * hh + HALF)
                    mm = split_product(ps_y[:, q], (w_hi[:, 0, :], w_lo[:, 0, :]), (g2_hi[:, q], g2_lo[:, q]),
                                       True, True)
                mm.then_inc(s["y_mm"], 1)

            def last_products():
                n = N - 1
                pixels = [h[:, :].rearrange("p (i a j b) -> p a b i j", a=2, b=2, i=J) for h in (g2_hi, g2_lo)]
                pe.wait_ge(s["g2_hi"], N)
                pe.wait_ge(s["z_ev"], n)
                for q in range(4):
                    for w in (w_hi, w_lo):
                        pe.matmul(ps_z[:, 0:J * J], w[:, 1 + q, :], pixels[0][:, q // 2, q % 2],
                                  start=(q == 0 and w is w_hi), stop=False)
                pe.wait_ge(s["g2_lo"], N)
                for q in range(4):
                    mm = pe.matmul(ps_z[:, 0:J * J], w_hi[:, 1 + q, :], pixels[1][:, q // 2, q % 2],
                                   start=False, stop=(q == 3))
                mm.then_inc(s["z_mm"], 1)
                y_product(n)

            for k in range(3):
                t5_product(k)
            for t in range(N + 2):
                if 1 <= t <= N:
                    out_product(t - 1)
                if t == 0:
                    keep_clock(2, ps_y)
                if t < N:
                    t6_transpose(t)
                if t == 0:
                    keep_clock(2, ps_y)
                if 3 <= t + 2 <= N:
                    t5_product(t + 2)
                if t == N + 1:
                    keep_clock(WARM_LAST, ps_t6)
                if t == N + 1:
                    last_products()
                    continue
                if t >= 2:
                    z_product(t - 2)
                if 1 <= t <= N:
                    group_average(t - 1)
                if t >= 2:
                    y_product(t - 2)

        @block.vector
        def _(dve):
            link = chained(dve, "dve")

            def t1_low(i):
                dve.wait_ge(s["t1_hi"], i + 1)
                q = t1_hi[:, :, 2:2 + J, (i - 1) % NO].bitcast(F32).rearrange("p g j -> p j g")
                dve.tensor_tensor(t1_lo[:, :, 2:2 + J, (i - 1) % NO].rearrange("p g j -> p j g"),
                                  ps_t1[i % 2][:, :].rearrange("p (j g) -> p j g", g=G), q,
                                  ALU.subtract).then_inc(s["t1_lo"], 1)

            def x_statistics(n, hh):
                dve.bn_stats(st1[:, n, 6 * hh:6 * hh + 6],
                             x_ring[:, n // 2 % XR, n % 2, HALF * hh:HALF * hh + HALF]).then_inc(s["x_used"], 1)

            for n in range(N):
                if n % 2 == 0:
                    dve.wait_ge(x_in[n // 2], 16 * CI)
                if n >= 2:
                    dve.wait_ge(s["t1_mm"], n)
                dve.transpose(xa[:, n % 2], x_ring[:, n // 2 % XR, n % 2, :].rearrange("p (h w) -> p w h", w=W)
                              ).then_inc(s["xa"], 1)
                if n < N - LATE:
                    for hh in range(2):
                        x_statistics(n, hh)
                if n == 1:
                    dve.wait_ge(s["p3_hi"], 1)
                    dve.tensor_tensor(p3_lo[:, :], p3_rows[:, :], p3_hi[:, :].bitcast(F32),
                                      ALU.subtract).then_inc(s["p3_lo"], 1)
                if n >= 1 and n - 1 not in LO_BY_POOL:
                    t1_low(n - 1)

            def split_low(g):
                dve.wait_ge(s["s_hi"], g + 1)
                if g >= 2:
                    dve.wait_ge(s["conv"], g - 1)
                if g >= 4:
                    dve.wait_ge(s["t4_mm"], g - 3)
                dve.tensor_tensor(s3_lo[:, g % 2, :], s3_f[:, g % 2].rearrange("p s c m -> p (s c m)"),
                                  s3_hi[:, g % 2, :].bitcast(F32), ALU.subtract)
                dve.tensor_tensor(s4_lo[:, g % 4, :], s4_f[:, g % 4].rearrange("p c v m -> p (c v m)"),
                                  s4_hi[:, g % 4, :].bitcast(F32), ALU.subtract).then_inc(s["s_lo"], 1)

            if N - 1 not in LO_BY_POOL:
                t1_low(N - 1)
            if N not in LO_BY_POOL:
                t1_low(N)
            split_low(0)
            for g in range(G):
                if g + 1 < G:
                    split_low(g + 1)
                dve.wait_ge(s["t3_hi"], g + 1)
                dve.tensor_tensor(t3_lo[:, g % 2, :], ps_t3[g % 2], t3_hi[:, g % 2, :].bitcast(F32),
                                  ALU.subtract).then_inc(s["t3_lo"], 1)
                if g < 2 * LATE:
                    x_statistics(N - LATE + g // 2, g % 2)
                elif g < 2 * LATE + N // 2:
                    if g == 2 * LATE:
                        dve.wait_ge(s["x_used"], 2 * N)
                    for n in (2 * (g - 2 * LATE), 2 * (g - 2 * LATE) + 1):
                        link(dve.bn_aggr(mv1[:, n, :], st1[:, n, :]))
                elif g == GST_AT:
                    link(dve.tensor_tensor(rs1[:, 0, :], mv1[:, :, 0], mv1[:, :, 0], ALU.mult))
                    dve.tensor_tensor(mv1[:, :, 1], mv1[:, :, 1], rs1[:, 0, :], ALU.add).then_inc(s["st1"], 1)
                elif g == GST_AT + 2:
                    dve.wait_ge(s["gst_mm"], 1)
                    link(dve.tensor_copy(gs1[:, :, :].rearrange("p n a -> p (n a)"), ps_st[:, 0:2 * N]))
                    link(dve.tensor_tensor(rs1[:, 0, :], gs1[:, :, 0], gs1[:, :, 0], ALU.mult))
                    link(dve.tensor_tensor(rs1[:, 0, :], gs1[:, :, 1], rs1[:, 0, :], ALU.subtract))
                    dve.tensor_scalar(rs1[:, 0, :], rs1[:, 0, :], 0.0, GN_EPS, ALU.max, ALU.add).then_inc(s["gst"], 1)
            dve.wait_ge(s["gst_q"], 1)
            link(dve.scalar_tensor_tensor(rs1[:, 2, :], gs1[:, :, 0], -1.0, rs1[:, 1, :], ALU.mult, ALU.mult))
            dve.wait_ge(s["p6_in"], 16 * 3 * CI)
            link(dve.tensor_scalar(p6_sb[:, :], p6_sb[:, :], float(NF) ** -0.5, None, ALU.mult))
            for d in range(3):
                last = dve.tensor_scalar(a6[:, d, :], rs1[:, 1, :], p6_sb[:, d:d + 1], None, ALU.mult)
            last.then_inc(s["rs1"], 1)

            for i in range(2):
                q = slice(2 * i, 2 * i + 2)
                dve.wait_ge(s["p5_first_hi"], i + 1)
                dve.tensor_tensor(p5_first[1][:, q, :], p5_sb[:, q, :], p5_first[0][:, q, :].bitcast(F32),
                                  ALU.subtract).then_inc(s["p5_first_lo"], 1)
            for i, (b, n0, n1, by_pool) in enumerate(SPLITS):
                if not by_pool:
                    dve.wait_ge(s["d_hi"], i + 1)
                    src, hi, lo = split_views(b, n0, n1)
                    dve.tensor_tensor(lo, src, hi.bitcast(F32), ALU.subtract).then_inc(s["d_lo"], 1)

            def u_views(k):
                dst = q6[:, :] if k == 0 else u_sb[:, k % 2, :]
                return dst, *(p6_sb[:, d:d + 1] if k == 0 else a6[:, d, k - 1:k] for d in (0, 2))

            def u_previous(k):
                dst, tap, _ = u_views(k)
                dve.wait_ge(s["u_act"], k + 1)
                for to, n, frm in ((C, 2 * C, 0), (G, 3 * G, 2 * C), (1, G - 1, 3 * C - G)):
                    ins = dve.scalar_tensor_tensor(dst[:, to:to + n], t5_bank(k)[:, frm:frm + n], tap,
                                                   dst[:, to:to + n], ALU.mult, ALU.add)
                ins.then_inc(s["u_part"], 1)

            def u_next(k):
                dst, _, tap = u_views(k)
                dve.wait_ge(s["u_part"], max(1, 2 * k))
                for to, n, frm in ((0, 2 * C, C), (2 * C, 3 * G, G), (3 * C - G, G - 1, 1)):
                    ins = dve.scalar_tensor_tensor(dst[:, to:to + n], t5_bank(k)[:, frm:frm + n], tap,
                                                   dst[:, to:to + n], ALU.mult, ALU.add)
                ins.then_inc(s["u_part"] if k else s["u"], 1)

            def u_mean(k):
                dst, _, _ = u_views(k)
                dve.wait_ge(s["u_part"], 2 * k + 1)
                if k == 1:
                    dve.wait_ge(s["u"], 1)
                dve.scalar_tensor_tensor(dst, q6[:, :], rs1[:, 2, k - 1:k], dst, ALU.mult, ALU.add
                                         ).then_inc(s["u"], 1)

            def x1_add(n, hh):
                sl = slice(HALF * hh, HALF * hh + HALF)
                dve.wait_ge(s["g1_f"], n + 1)
                dve.wait_ge(s["o_mm"] if hh else s["o_half"], n + 1)
                dve.tensor_tensor(x_sb[:, n, sl], x_sb[:, n, sl], ps_o[:, sl], ALU.add).then_inc(s["x1"], 1)

            def x1_statistics(n):
                b = n % 2
                for hh in range(2):
                    dve.wait_ge(s["x1"], 2 * n + hh + 1)
                    ins = dve.bn_stats(st2[:, b, 6 * hh:6 * hh + 6], x_sb[:, n, HALF * hh:HALF * hh + HALF])
                link(ins)
                link(dve.bn_aggr(mv2[:, b, :], st2[:, b, :]))
                dve.scalar_tensor_tensor(mv2[:, b, 1:2], mv2[:, b, 0:1], mv2[:, b, 0:1], mv2[:, b, 1:2],
                                         ALU.mult, ALU.add).then_inc(s["st2"], 1)

            def t6_low(n):
                dve.wait_ge(s["t6_hi"], n + 1)
                dve.tensor_tensor(t6_lo[:, :, :], ps_t6[:, 0:NF].rearrange("p (k c) -> p k c", k=3),
                                  t6_hi[:, :, :].bitcast(F32), ALU.subtract).then_inc(s["t6_lo"], 1)

            def y_views(n):
                return (v.rearrange("p (i a w) -> p a i w", a=2, w=W) for v in (y_sb[:, n, :], ps_y[:, :]))

            def y_neighbours(n):
                yr, pr = y_views(n)
                dve.wait_ge(s["zh"], n + 1)
                dve.wait_ge(s["y_mm"], n + 1)
                for a in range(2):
                    ins = dve.tensor_tensor(yr[:, a], pr[:, a], zh[:, n % 2, 2 * a:2 * a + J, :], ALU.add)
                ins.then_inc(s["y_rd"], 1)

            def y_own(n):
                yr, _ = y_views(n)
                dve.wait_ge(s["y_rd"], n + 1)
                for a in range(2):
                    ins = dve.scalar_tensor_tensor(yr[:, a], zh[:, n % 2, 1:J + 1, :], 3.0, yr[:, a],
                                                   ALU.mult, ALU.add)
                ins.then_inc(s["y"], 1)

            def y_statistics(n, hh):
                dve.wait_ge(s["y"], n + 1)
                dve.bn_stats(sty[:, n, 6 * hh:6 * hh + 6],
                             y_sb[:, n, HALF * hh:HALF * hh + HALF]).then_inc(s["sty"], 1)

            def g1_low_first():
                dve.wait_ge(s["g1_hi"], 1)
                dve.tensor_tensor(g1_lo[:, W:W + HW], y_sb[:, 0, :], g1_hi[:, W:W + HW].bitcast(F32),
                                  ALU.subtract).then_inc(s["g1_lo"], 1)

            def g2_low_last():
                dve.wait_ge(s["g2_hi"], N)
                dve.tensor_tensor(g2_lo[:, :], y_sb[:, N - 1, :], g2_hi[:, :].bitcast(F32),
                                  ALU.subtract).then_inc(s["g2_lo"], 1)

            u_previous(0)
            u_next(0)
            u_previous(1)
            u_next(1)
            u_mean(1)
            g1_low_first()
            for t in range(N + 3):
                if 1 <= t <= N:
                    x1_add(t - 1, 0)
                if t == N + 1:
                    g2_low_last()
                if t >= 3:
                    y_neighbours(t - 3)
                if 1 <= t <= N:
                    x1_add(t - 1, 1)
                    x1_statistics(t - 1)
                if t < N:
                    t6_low(t)
                y, u = t - 3, t + 2
                if u <= N:
                    u_previous(u)
                if y >= 0:
                    y_own(y)
                if u <= N:
                    u_next(u)
                if y >= 0:
                    y_statistics(y, 0)
                if u <= N:
                    u_mean(u)
                if y >= 0:
                    y_statistics(y, 1)
            dve.wait_ge(s["sty"], 2 * N)
            link(dve.bn_aggr(fin[:, 1:3], sty[:, :, :].rearrange("p n a -> p (n a)")))
            dve.tensor_scalar(fin[:, 2:3], fin[:, 2:3], 0.0, BN_EPS, ALU.max, ALU.add).then_inc(s["fin_s"], 1)
            dve.wait_ge(s["fin_q"], 1)
            link(dve.tensor_tensor(fin[:, 5:6], fin[:, 4:5], gb[:, 0:1], ALU.mult))
            link(dve.tensor_tensor(fin[:, 7:8], fin[:, 1:2], fin[:, 5:6], ALU.mult))
            dve.tensor_tensor(fin[:, 6:7], gb[:, 1:2], fin[:, 7:8], ALU.subtract).then_inc(s["fin"], 1)
            for i, (n, sl) in enumerate(PIECES):
                dve.wait_ge(s["relu"], i + 1)
                dve.tensor_tensor(x_sb[:, n, sl], x_sb[:, n, sl], y_sb[:, n, sl], ALU.add).then_inc(s["res"], 1)


INPUTS = {"x": "x", "p1": "L0_conv_p1", "p3": "L0_conv_p3", "p4": "L0_conv_p4", "p5": "L0_conv_p5",
          "p6": "L0_conv_p6", "conv_w": "L1_conv_conv_w", "gamma": "L1_conv_gamma", "beta": "L1_conv_beta"}


def kernel(x, L0_conv_p1, L0_conv_p3, L0_conv_p4, L0_conv_p5, L0_conv_p6, L1_conv_conv_w, L1_conv_gamma,
           L1_conv_beta):
    import numpy as np
    import concourse.bacc as bacc
    from concourse.bass_utils import run_bass_kernel_spmd

    given = [x, L0_conv_p1, L0_conv_p3, L0_conv_p4, L0_conv_p5, L0_conv_p6, L1_conv_conv_w, L1_conv_gamma,
             L1_conv_beta]
    nc = bacc.Bacc("TRN2", target_bir_lowering=False, num_devices=1)
    arrays = {"in_" + k: np.ascontiguousarray(v) for k, v in zip(INPUTS, given)}
    args = [nc.dram_tensor(k, v.shape, mybir.dt.from_np(v.dtype), kind="ExternalInput").ap()
            for k, v in arrays.items()]
    out = nc.dram_tensor("out", (N, C, H, W), F32, kind="ExternalOutput").ap()
    build(nc, *args, out)
    result = run_bass_kernel_spmd(nc, [arrays], core_ids=[0])
    return result.results[0]["out"]
```
